# Optimizing a Trainium2 kernel written in Bass

```python
import numpy as np
import jax
import jax.numpy as jnp

def _softmax(x, axis=-1):
    return jax.nn.softmax(x, axis=axis)

def _gelu(x):
    return jax.nn.gelu(x, approximate=True)

def _silu(x):
    return jax.nn.silu(x)

def _sigmoid(x):
    return jax.nn.sigmoid(x)

def _layernorm(x, axis=-1, eps=1e-05):
    m = jnp.mean(x, axis=axis, keepdims=True)
    v = jnp.var(x, axis=axis, keepdims=True)
    return (x - m) / jnp.sqrt(v + eps)

def _scatter_add(tgt, idx, src, axis=0):
    return tgt.at[idx].add(src)

def _segment_sum(src, seg, n):
    return jax.ops.segment_sum(src, seg, n)
kernel_name = 'mk_xattn_seq_d2_seqx_r2_98df86'

def setup_inputs(seed: int=0):
    np.random.seed(seed)
    _w = jnp.asarray

    def _rec_inputs():
        import jax
        import jax.numpy as jnp
        _rk = jax.random.key(seed)
        x = -0.0002928 + 1 * jax.random.normal(jax.random.fold_in(_rk, 1), (16, 256, 512), jnp.float32)
        _lenS = 256 - jax.random.randint(jax.random.fold_in(_rk, 7), (16,), 0, max(1, 256 // 4) + 1, jnp.int32)
        _lenS2 = 256 - jax.random.randint(jax.random.fold_in(_rk, 8), (16,), 0, max(1, 256 // 4) + 1, jnp.int32)
        _ctx_1024P = jax.random.normal(jax.random.fold_in(_rk, 11), (16, 16, 512), jnp.float32)
        _ctx_1024c = jax.random.dirichlet(jax.random.fold_in(_rk, 511), 0.3 * jnp.ones((16,), jnp.float32), (16, 256))
        _ctx_1024t = jnp.einsum('bsk,bkd->bsd', _ctx_1024c, _ctx_1024P)
        _ctx_1024t = _ctx_1024t * jax.lax.rsqrt(jnp.mean(jnp.square(_ctx_1024t)) + 1e-12) * 0.953939
        ctx_1024 = -1.39393e-06 + 0.999914 * (_ctx_1024t + 0.3 * jax.random.normal(jax.random.fold_in(_rk, 611), (16, 256, 512), jnp.float32))
        _validS = jnp.arange(256)[None, :] < _lenS[:, None]
        _validS2 = jnp.arange(256)[None, :] < _lenS2[:, None]
        _causal = jnp.tril(jnp.ones((256, 256), dtype=bool))
        mask_BxSxS2_bk0 = jnp.logical_not(jnp.broadcast_to(_validS2[:, None, :], (16, 256, 256)))
        return (x, ctx_1024, mask_BxSxS2_bk0)
    x, ctx_1024, mask_BxSxS2_bk0 = _rec_inputs()

    def _L0_xattn_setup():
        import jax, jax.numpy as jnp
        import numpy as np
        EPS = 1e-05

        def layer_norm(x, w, b):
            mu = jnp.mean(x, axis=-1, keepdims=True)
            var = jnp.var(x, axis=-1, keepdims=True)
            return (x - mu) * jax.lax.rsqrt(var + EPS) * w + b
        key = jax.random.key(seed)
        ks = jax.random.split(key, 12)
        B, N, M, C = (2, 1024, 1024, 512)
        H = 16
        hid = 4 * C
        s = lambda d: 1.0 / np.sqrt(d)
        return {'x': jax.random.normal(ks[0], (B, N, C), jnp.float32), 'context': jax.random.normal(ks[1], (B, M, C), jnp.float32), 'xa_mask': jax.random.bernoulli(ks[2], 0.1, (B, N, M)), 'qn_w': jnp.ones((C,), jnp.float32), 'qn_b': jnp.zeros((C,), jnp.float32), 'cn_w': jnp.ones((C,), jnp.float32), 'cn_b': jnp.zeros((C,), jnp.float32), 'n2_w': jnp.ones((C,), jnp.float32), 'n2_b': jnp.zeros((C,), jnp.float32), 'q_w': jax.random.normal(ks[3], (C, C), jnp.float32) * s(C), 'kv_w': jax.random.normal(ks[4], (C, 2 * C), jnp.float32) * s(C), 'proj_w': jax.random.normal(ks[5], (C, C), jnp.float32) * s(C), 'proj_b': jnp.zeros((C,), jnp.float32), 'fc1_w': jax.random.normal(ks[6], (C, hid), jnp.float32) * s(C), 'fc1_b': jnp.zeros((hid,), jnp.float32), 'fc2_w': jax.random.normal(ks[7], (hid, C), jnp.float32) * s(hid), 'fc2_b': jnp.zeros((C,), jnp.float32)}
    _L0_xattn_all = _L0_xattn_setup()
    _L0_xattn_in = {k: v for k, v in _L0_xattn_all.items() if k in ('qn_w', 'qn_b', 'cn_w', 'cn_b', 'n2_w', 'n2_b', 'q_w', 'kv_w', 'proj_w', 'proj_b', 'fc1_w', 'fc1_b', 'fc2_w', 'fc2_b')}
    del _L0_xattn_all

    def _L1_xattn_setup():
        import jax, jax.numpy as jnp
        import numpy as np
        EPS = 1e-05

        def _layernorm(x, g, b):
            m = jnp.mean(x, axis=-1, keepdims=True)
            v = jnp.mean((x - m) ** 2, axis=-1, keepdims=True)
            return (x - m) / jnp.sqrt(v + EPS) * g + b

        def _mha(x, kv, Wq, Wk, Wv, mask, causal):
            m = mask[:, None]
            Q = jnp.einsum('bsd,hdk->bhsk', x, Wq) * m
            K = jnp.einsum('bsd,hdk->bhsk', kv, Wk) * m
            V = jnp.einsum('bsd,hdk->bhsk', kv, Wv) * m
            energy = jnp.einsum('bhsk,bhtk->bhst', Q, K)
            S = energy.shape[-1]
            lengths = jnp.sum(energy[:, :, 0, :] != 0, axis=-1)
            cols = jnp.arange(S)
            energy = jnp.where(cols[None, None, None, :] >= lengths[:, :, None, None], -jnp.inf, energy)
            if causal:
                energy = jnp.where(cols[None, :] > cols[:, None], -jnp.inf, energy)
            dk = Wq.shape[-1]
            score = jax.nn.softmax(energy / jnp.sqrt(jnp.asarray(dk, energy.dtype)), axis=-1)
            out = jnp.einsum('bhst,bhtk->bhsk', score, V) * m
            B, H, Sx, dkk = out.shape
            return out.transpose(0, 2, 1, 3).reshape(B, Sx, H * dkk)
        key = jax.random.key(seed)
        ks = jax.random.split(key, 20)
        B, S, D, H = (2, 1024, 512, 16)
        dk = D // H
        sd = 0.02
        inp = {'x': jax.random.normal(ks[0], (B, S, D), jnp.float32), 'context': jax.random.normal(ks[1], (B, S, D), jnp.float32), 'Wq1': jax.random.normal(ks[2], (H, D, dk), jnp.float32) * sd, 'Wk1': jax.random.normal(ks[3], (H, D, dk), jnp.float32) * sd, 'Wv1': jax.random.normal(ks[4], (H, D, dk), jnp.float32) * sd, 'Wq2': jax.random.normal(ks[5], (H, D, dk), jnp.float32) * sd, 'Wk2': jax.random.normal(ks[6], (H, D, dk), jnp.float32) * sd, 'Wv2': jax.random.normal(ks[7], (H, D, dk), jnp.float32) * sd, 'ln1_g': jnp.ones((D,), jnp.float32), 'ln1_b': jnp.zeros((D,), jnp.float32), 'ln2_g': jnp.ones((D,), jnp.float32), 'ln2_b': jnp.zeros((D,), jnp.float32), 'ln3_g': jnp.ones((D,), jnp.float32), 'ln3_b': jnp.zeros((D,), jnp.float32), 'fc1_w': jax.random.normal(ks[8], (D, D), jnp.float32) * sd, 'fc1_b': jnp.zeros((D,), jnp.float32), 'fc2_w': jax.random.normal(ks[9], (D, D), jnp.float32) * sd, 'fc2_b': jnp.zeros((D,), jnp.float32)}
        return inp
    _L1_xattn_all = _L1_xattn_setup()
    _L1_xattn_in = {k: v for k, v in _L1_xattn_all.items() if k in ('Wq1', 'Wk1', 'Wv1', 'Wq2', 'Wk2', 'Wv2', 'ln1_g', 'ln1_b', 'ln2_g', 'ln2_b', 'ln3_g', 'ln3_b', 'fc1_w', 'fc1_b', 'fc2_w', 'fc2_b')}
    del _L1_xattn_all
    return {'x': x, 'ctx_1024': ctx_1024, 'mask_BxSxS2_bk0': mask_BxSxS2_bk0, 'L0_xattn_qn_w': _L0_xattn_in['qn_w'], 'L0_xattn_qn_b': _L0_xattn_in['qn_b'], 'L0_xattn_cn_w': _L0_xattn_in['cn_w'], 'L0_xattn_cn_b': _L0_xattn_in['cn_b'], 'L0_xattn_n2_w': _L0_xattn_in['n2_w'], 'L0_xattn_n2_b': _L0_xattn_in['n2_b'], 'L0_xattn_q_w': _L0_xattn_in['q_w'], 'L0_xattn_kv_w': _L0_xattn_in['kv_w'], 'L0_xattn_proj_w': _L0_xattn_in['proj_w'], 'L0_xattn_proj_b': _L0_xattn_in['proj_b'], 'L0_xattn_fc1_w': _L0_xattn_in['fc1_w'], 'L0_xattn_fc1_b': _L0_xattn_in['fc1_b'], 'L0_xattn_fc2_w': _L0_xattn_in['fc2_w'], 'L0_xattn_fc2_b': _L0_xattn_in['fc2_b'], 'L1_xattn_Wq1': _L1_xattn_in['Wq1'], 'L1_xattn_Wk1': _L1_xattn_in['Wk1'], 'L1_xattn_Wv1': _L1_xattn_in['Wv1'], 'L1_xattn_Wq2': _L1_xattn_in['Wq2'], 'L1_xattn_Wk2': _L1_xattn_in['Wk2'], 'L1_xattn_Wv2': _L1_xattn_in['Wv2'], 'L1_xattn_ln1_g': _L1_xattn_in['ln1_g'], 'L1_xattn_ln1_b': _L1_xattn_in['ln1_b'], 'L1_xattn_ln2_g': _L1_xattn_in['ln2_g'], 'L1_xattn_ln2_b': _L1_xattn_in['ln2_b'], 'L1_xattn_ln3_g': _L1_xattn_in['ln3_g'], 'L1_xattn_ln3_b': _L1_xattn_in['ln3_b'], 'L1_xattn_fc1_w': _L1_xattn_in['fc1_w'], 'L1_xattn_fc1_b': _L1_xattn_in['fc1_b'], 'L1_xattn_fc2_w': _L1_xattn_in['fc2_w'], 'L1_xattn_fc2_b': _L1_xattn_in['fc2_b']}

def reference(x, ctx_1024, mask_BxSxS2_bk0, L0_xattn_qn_w, L0_xattn_qn_b, L0_xattn_cn_w, L0_xattn_cn_b, L0_xattn_n2_w, L0_xattn_n2_b, L0_xattn_q_w, L0_xattn_kv_w, L0_xattn_proj_w, L0_xattn_proj_b, L0_xattn_fc1_w, L0_xattn_fc1_b, L0_xattn_fc2_w, L0_xattn_fc2_b, L1_xattn_Wq1, L1_xattn_Wk1, L1_xattn_Wv1, L1_xattn_Wq2, L1_xattn_Wk2, L1_xattn_Wv2, L1_xattn_ln1_g, L1_xattn_ln1_b, L1_xattn_ln2_g, L1_xattn_ln2_b, L1_xattn_ln3_g, L1_xattn_ln3_b, L1_xattn_fc1_w, L1_xattn_fc1_b, L1_xattn_fc2_w, L1_xattn_fc2_b):
    import jax
    import jax.numpy as jnp

    def _L0_xattn_ref(x, context, xa_mask, qn_w, qn_b, cn_w, cn_b, n2_w, n2_b, q_w, kv_w, proj_w, proj_b, fc1_w, fc1_b, fc2_w, fc2_b):
        import jax, jax.numpy as jnp
        import numpy as np
        EPS = 1e-05

        def layer_norm(x, w, b):
            mu = jnp.mean(x, axis=-1, keepdims=True)
            var = jnp.var(x, axis=-1, keepdims=True)
            return (x - mu) * jax.lax.rsqrt(var + EPS) * w + b
        B, N, C = x.shape
        M = context.shape[1]
        H = 16
        D = C // H
        scale = D ** (-0.5)
        xq = layer_norm(x, qn_w, qn_b)
        ctx = layer_norm(context, cn_w, cn_b)
        q = (xq @ q_w).reshape(B, N, H, D)
        kv = (ctx @ kv_w).reshape(B, M, 2, H, D)
        k, v = (kv[:, :, 0], kv[:, :, 1])
        attn = jnp.einsum('bnhd,bmhd->bhnm', q, k) * scale
        neg = -jnp.finfo(attn.dtype).max
        attn = jnp.where(xa_mask[:, None, :, :], neg, attn)
        attn = jax.nn.softmax(attn, axis=-1)
        out = jnp.einsum('bhnm,bmhd->bnhd', attn, v).reshape(B, N, C)
        out = out @ proj_w + proj_b
        x = x + out
        h = layer_norm(x, n2_w, n2_b)
        h = jax.nn.gelu(h @ fc1_w + fc1_b, approximate=False) @ fc2_w + fc2_b
        return x + h

    def _L1_xattn_ref(x, context, Wq1, Wk1, Wv1, Wq2, Wk2, Wv2, ln1_g, ln1_b, ln2_g, ln2_b, ln3_g, ln3_b, fc1_w, fc1_b, fc2_w, fc2_b):
        import jax, jax.numpy as jnp
        import numpy as np
        EPS = 1e-05

        def _layernorm(x, g, b):
            m = jnp.mean(x, axis=-1, keepdims=True)
            v = jnp.mean((x - m) ** 2, axis=-1, keepdims=True)
            return (x - m) / jnp.sqrt(v + EPS) * g + b

        def _mha(x, kv, Wq, Wk, Wv, mask, causal):
            m = mask[:, None]
            Q = jnp.einsum('bsd,hdk->bhsk', x, Wq) * m
            K = jnp.einsum('bsd,hdk->bhsk', kv, Wk) * m
            V = jnp.einsum('bsd,hdk->bhsk', kv, Wv) * m
            energy = jnp.einsum('bhsk,bhtk->bhst', Q, K)
            S = energy.shape[-1]
            lengths = jnp.sum(energy[:, :, 0, :] != 0, axis=-1)
            cols = jnp.arange(S)
            energy = jnp.where(cols[None, None, None, :] >= lengths[:, :, None, None], -jnp.inf, energy)
            if causal:
                energy = jnp.where(cols[None, :] > cols[:, None], -jnp.inf, energy)
            dk = Wq.shape[-1]
            score = jax.nn.softmax(energy / jnp.sqrt(jnp.asarray(dk, energy.dtype)), axis=-1)
            out = jnp.einsum('bhst,bhtk->bhsk', score, V) * m
            B, H, Sx, dkk = out.shape
            return out.transpose(0, 2, 1, 3).reshape(B, Sx, H * dkk)
        mask0 = 1.0 - jnp.all(x == 0, axis=2, keepdims=True).astype(x.dtype)
        z = _mha(x, x, Wq1, Wk1, Wv1, mask0, causal=True)
        x1 = _layernorm(x + z, ln1_g, ln1_b)
        mask1 = 1.0 - jnp.all(x1 == 0, axis=2, keepdims=True).astype(x1.dtype)
        z = _mha(x1, context, Wq2, Wk2, Wv2, mask1, causal=False)
        x2 = _layernorm(x1 + z, ln2_g, ln2_b)
        z = jnp.maximum(x2 @ fc1_w.T + fc1_b, 0.0) * mask0
        z = (z @ fc2_w.T + fc2_b) * mask0
        return _layernorm(x2 + z, ln3_g, ln3_b)
    x = _L0_xattn_ref(x, ctx_1024, mask_BxSxS2_bk0, L0_xattn_qn_w, L0_xattn_qn_b, L0_xattn_cn_w, L0_xattn_cn_b, L0_xattn_n2_w, L0_xattn_n2_b, L0_xattn_q_w, L0_xattn_kv_w, L0_xattn_proj_w, L0_xattn_proj_b, L0_xattn_fc1_w, L0_xattn_fc1_b, L0_xattn_fc2_w, L0_xattn_fc2_b)
    x = _L1_xattn_ref(x, ctx_1024, L1_xattn_Wq1, L1_xattn_Wk1, L1_xattn_Wv1, L1_xattn_Wq2, L1_xattn_Wk2, L1_xattn_Wv2, L1_xattn_ln1_g, L1_xattn_ln1_b, L1_xattn_ln2_g, L1_xattn_ln2_b, L1_xattn_ln3_g, L1_xattn_ln3_b, L1_xattn_fc1_w, L1_xattn_fc1_b, L1_xattn_fc2_w, L1_xattn_fc2_b)
    return x

_drawn_inputs = setup_inputs


def setup_inputs(seed=0):
    import zlib

    import numpy as np

    out = dict(_drawn_inputs(seed))
    spreads = {'L0_xattn_qn_w': (1.0, 0.2),
     'L0_xattn_qn_b': (0.0, 0.458),
     'L0_xattn_cn_w': (1.0, 0.2),
     'L0_xattn_cn_b': (0.0, 0.1),
     'L0_xattn_n2_w': (1.0, 0.2),
     'L0_xattn_n2_b': (0.0, 0.1),
     'L0_xattn_proj_b': (0.0, 0.1),
     'L0_xattn_fc1_b': (0.0, 0.1),
     'L0_xattn_fc2_b': (0.0, 0.1),
     'L1_xattn_ln1_g': (1.0, 0.2),
     'L1_xattn_ln1_b': (0.0, 0.1),
     'L1_xattn_ln2_g': (1.0, 0.2),
     'L1_xattn_ln2_b': (0.0, 0.1),
     'L1_xattn_ln3_g': (1.0, 0.2),
     'L1_xattn_ln3_b': (0.0, 0.1),
     'L1_xattn_fc1_b': (0.0, 0.1),
     'L1_xattn_fc2_b': (0.0, 0.1)}
    factors = {'L1_xattn_Wq1': 3.451, 'L1_xattn_Wk1': 3.424, 'L1_xattn_Wq2': 3.525, 'L1_xattn_Wk2': 3.55}
    for name, (base, spread) in spreads.items():
        noise = np.random.default_rng([zlib.crc32(name.encode()), seed]).standard_normal(out[name].shape)
        drawn = base * np.exp(spread * noise) if base else spread * noise
        out[name] = jnp.asarray(drawn.astype(out[name].dtype))
    for name, factor in factors.items():
        out[name] = (out[name] * factor).astype(out[name].dtype)
    return out
```

```python
from contextlib import ExitStack

import numpy as np

import concourse.bass as bass
from concourse import mybir

F32 = mybir.dt.float32
F32R = mybir.dt.float32r
BF16 = mybir.dt.bfloat16
I32 = mybir.dt.int32
U8 = mybir.dt.uint8
ALU = mybir.AluOpType
ACT = mybir.ActivationFunctionType
AX_X = mybir.AxisListType.X

P = 128
B, S, C = 16, 256, 512
H = 16
DH = C // H
KC = C // P
HC = P // DH
TT = S // P
HID = 4 * C
EPS = 1e-5
SCALE = float(DH) ** -0.5
F32_MAX = float(np.finfo(np.float32).max)
BIG = 3e38
BEYOND = 60000.0
UNITS = KC * TT * 2
IT = 16


class Chain:

    def __init__(self, eng, sem, head, per):
        self.eng, self.sem, self.head, self.per = eng, sem, head, per
        self.base, self.k, self.entered = 0, 0, False

    def turn(self, b):
        want = self.per if self.entered else self.head
        assert self.k == want, (self.sem, "steps", self.k, "of", want)
        self.entered = True
        self.base, self.k = self.head + b * self.per, 0

    def done(self, ins):
        ins.then_inc(self.sem, 1)
        self.k += 1

    def wait(self):
        self.eng.wait_ge(self.sem, self.base + self.k)

    def hold(self, s):
        hold(self.eng, self.sem, self.base + self.k, s)


def rows(m):
    return m.rearrange("(k p) n -> p k n", p=P)


def tokens(t, b):
    return t[bass.ds(b, 1)].rearrange("o (t p) c -> p (o t) c", p=P)


def hold(eng, sem, value, s):
    eng.wait_ge(sem, value)
    eng.sem_inc(s["held"], 1)


class Signals(dict):

    def __init__(self, nc, phase):
        super().__init__()
        self.nc, self.phase = nc, phase

    def __missing__(self, name):
        self[name] = self.nc.alloc_semaphore(f"{self.phase}_{name}")
        return self[name]

    def close(self):
        self.nc.clear_and_free_semaphores(list(self.values()))
        self.nc.all_engine_barrier()


PASSES = ((0, 0), (0, 1), (1, 0))


def product(pe, out, lhs, rhs):
    last = None
    n = 0
    for k in range(KC):
        for a, c in PASSES:
            last = pe.matmul(out, lhs(k, a), rhs(k, c), start=(n == 0), stop=(n == KC * len(PASSES) - 1))
            n += 1
    return last


def attention_phase(nc, kind, x_src, ctx_src, mask_src, dst, mats, vecs, keep):
    masked_ctx, causal, cross = kind == "mask", kind == "causal", kind == "cross"
    lengths = not masked_ctx
    two = not causal
    NP = 4 if two else 2
    NM = len(mats)

    with ExitStack() as ctx:
        def sb(name, shape, dt=F32):
            return ctx.enter_context(nc.sbuf_tensor(f"{kind}_{name}", shape, dt))

        def bank(name, dt=F32):
            return ctx.enter_context(nc.psum_tensor(f"{kind}_{name}", [P, 512], dt))

        W = [sb(f"w_{part}", [P, NM, KC, C], F32R) for part in ("hi", "lo")]
        stage = sb("stage", [P, 2, KC, C])
        ident = sb("ident", [P, P])
        x_in = sb("x_in", [P, TT, C])
        res = sb("res", [P, TT, C])
        z = sb("z", [P, TT, C])
        xT = [sb(f"xT_{part}", [P, KC, S], F32R) for part in ("hi", "lo")]
        if two:
            c_in = sb("c_in", [P, TT, C])
            cT = [sb(f"cT_{part}", [P, KC, S], F32R) for part in ("hi", "lo")]
        else:
            cT = xT
        Q = [sb(f"q_{part}", [P, 2, S], F32R) for part in ("hi", "lo")]
        K = [sb(f"k_{part}", [P, 2, HC, S], F32R) for part in ("hi", "lo")]
        K32 = sb("k32", [P, S])
        V = sb("v", [P, TT, H, DH + 1])
        prob = sb("prob", [P, 3, 2, S])
        probT = sb("probT", [P, 3, 512])
        low = sb("low", [P, 3, 2])
        rs = sb("rs", [P, TT, HC])
        if masked_ctx:
            m_in = sb("m_in", [P, TT, S], U8)
            mask = sb("mask", [P, TT, S])
            wcol = sb("wcol", [P, 4, KC])
            wq_scale = sb("wq_scale", [P, KC])
            bias_rep = sb("bias_rep", [P, KC, P])
            qk_bias = sb("qk_bias", [P, 2, KC])
            v_bias = sb("v_bias", [P, C])
            p_bias = sb("p_bias", [P, C])
            stats = sb("stats", [P, 4, 6])
            mv = sb("mv", [P, 4, 2])
            rstd = sb("rstd", [P, 4])
            half = sb("half", [P, 4])
            zT = [sb(f"zT_{part}", [P, KC, S], F32R) for part in ("hi", "lo")]
        else:
            ones = sb("ones", [P, P], BF16)
            iota_i = sb("iota_i", [P, 3 * P if causal else S], I32)
            key = sb("key", [P, 3 * P if causal else S], BF16)
            head_of = sb("head_of", [P, HC])
            Q0 = sb("q0", [P, HC])
            flags = sb("flags", [P, TT, HC], BF16)
            lens = sb("lens", [P, HC])
            rlen = sb("rlen", [P, HC])
            nan0 = sb("nan0", [P, 2, HC])
            cut = sb("cut", [P, 2, HC, 3 * P if causal else S], BF16)
            big = sb("big", [P, TT])
            m_next = sb("m_next", [P, TT])
            m_cur = sb("m_cur", [P, TT])
            g_rep = sb("g_rep", [P, C])
            b_rep = sb("b_rep", [P, C])
            stats = sb("stats", [P, TT, 6])
            mv = sb("mv", [P, TT, 2])
            rstd = sb("rstd", [P, TT])
            half = sb("half", [P, TT])
        if cross:
            x2T = [sb(f"x2T_{part}", [P, KC, S], F32R) for part in ("hi", "lo")]
            h32 = sb("h32", [P, KC, S])
            hT = [sb(f"hT_{part}", [P, KC, S], F32R) for part in ("hi", "lo")]
            f1b = sb("f1b", [P, KC])
            f2b = sb("f2b", [P, C])
            g3 = sb("g3", [P, C])
            b3 = sb("b3", [P, C])
            m0 = sb("m0", [P, TT])

        SC = [bank(f"scores{i}") for i in range(3)]
        PT = [bank(f"probsT{i}") for i in range(2)]
        O = bank("attended")
        G = bank("qk")
        M = bank("small")
        TB = [G, M]
        Ov = O[:, 0:TT * HC * (DH + 1)].rearrange("p (t h d) -> p t h d", t=TT, h=HC)

        s = Signals(nc, kind)
        ctx.callback(s.close)

        def where_vecs():
            if masked_ctx:
                return [(wcol[:, i, :], (v)) for i, v in enumerate(vecs[0:4])] + [
                    (p_bias[:], vecs[4].partition_broadcast(P))]
            out = [(g_rep[:], vecs[0].partition_broadcast(P)), (b_rep[:], vecs[1].partition_broadcast(P))]
            if cross:
                out += [(f1b[:], (vecs[2])), (f2b[:], vecs[3].partition_broadcast(P)),
                        (g3[:], vecs[4].partition_broadcast(P)), (b3[:], vecs[5].partition_broadcast(P))]
            return out

        NV = len(where_vecs())
        block = ctx.enter_context(nc.Block())

        @block.sync
        def _(sp):
            for to, frm in where_vecs():
                sp.dma_start(to, frm).then_inc(s["vec_loaded"], IT)

            def load_inputs(b, first=False):
                if not first:
                    hold(sp, s["t_ps"], NP * b, s)
                    if lengths:
                        hold(sp, s["x_seen"], b, s)
                sp.dma_start(x_in[:], tokens(x_src, b)).then_inc(s["x_loaded"], IT)
                if two:
                    sp.dma_start(c_in[:], tokens(ctx_src, b)).then_inc(s["c_loaded"], IT)
                if masked_ctx:
                    if not first:
                        hold(sp, s["m_ready"], b, s)
                    sp.dma_start(m_in[:], mask_src[bass.ds(b, 1)].rearrange("o (t p) k -> p (o t) k", p=P)
                                 ).then_inc(s["m_loaded"], IT)

            load_inputs(0, first=True)
            for i, m in enumerate(mats):
                if i >= 2:
                    sp.wait_ge(s["w_hi_done"], i - 1)
                    sp.wait_ge(s["w_lo_done"], i - 1)
                    if masked_ctx and i - 2 < 3:
                        sp.wait_ge(s["bias_ps"], i - 1)
                sp.dma_start(stage[:, i % 2], rows(m)).then_inc(s[f"stage_loaded{i % 2}"], IT)

            def turn(b, last=False):
                sp.dma_start(res[:], tokens(x_src, b)).then_inc(s["res_loaded"], IT)
                if not last:
                    load_inputs(b + 1)
                hold(sp, s["out_ready"], b + 1, s)
                sp.dma_start(tokens(dst, b), res[:]).then_inc(s["stored"], IT)
                hold(sp, s["stored"], IT * (b + 1), s)

            with sp.Fori(0, B - 1) as b:
                turn(b)
            turn(B - 1, last=True)

        @block.gpsimd
        def _(pool):
            pool.memset(ident[:], 0.0).then_inc(s["pool_chain"], 1)
            pool.wait_ge(s["pool_chain"], 1)
            pool.affine_select(out=ident[:], in_=ident[:], compare_op=ALU.not_equal, fill=1.0, base=0,
                               pattern=[[-1, P]], channel_multiplier=1).then_inc(s["pool_setup"], 1)
            pool.memset(half[:], -0.5).then_inc(s["pool_chain"], 1)
            n = 2
            if lengths:
                pool.memset(head_of[:], 1.0).then_inc(s["head_chain"], 1)
                pool.wait_ge(s["head_chain"], 1)
                pool.affine_select(out=head_of[:], in_=head_of[:], compare_op=ALU.is_ge, fill=0.0, base=0,
                                   pattern=[[-DH, HC]], channel_multiplier=1).then_inc(s["head_chain"], 1)
                pool.wait_ge(s["head_chain"], 2)
                pool.affine_select(out=head_of[:], in_=head_of[:], compare_op=ALU.is_ge, fill=0.0, base=DH - 1,
                                   pattern=[[DH, HC]], channel_multiplier=-1).then_inc(s["pool_setup"], 1)
            if causal:
                pool.iota(iota_i[:, 0:P], pattern=[[1, P]], base=0, channel_multiplier=0).then_inc(s["pool_chain"], 1)
                pool.iota(iota_i[:, P:3 * P], pattern=[[1, S]], base=0, channel_multiplier=0
                          ).then_inc(s["pool_chain"], 1)
                pool.wait_ge(s["pool_chain"], 4)
                pool.tensor_copy(key[:], iota_i[:]).then_inc(s["pool_chain"], 1)
                pool.wait_ge(s["pool_chain"], 5)
                pool.affine_select(out=key[:, 0:P], in_=key[:, 0:P], compare_op=ALU.is_ge, fill=BEYOND, base=0,
                                   pattern=[[-1, P]], channel_multiplier=1).then_inc(s["pool_setup"], 1)
                pool.affine_select(out=key[:, P:3 * P], in_=key[:, P:3 * P], compare_op=ALU.is_ge, fill=BEYOND,
                                   base=P, pattern=[[-1, S]], channel_multiplier=1).then_inc(s["pool_setup"], 1)
                n = 5
            elif cross:
                pool.iota(iota_i[:], pattern=[[1, S]], base=0, channel_multiplier=0).then_inc(s["pool_chain"], 1)
                pool.wait_ge(s["pool_chain"], 3)
                pool.tensor_copy(key[:], iota_i[:]).then_inc(s["pool_setup"], 1)
                n = 3
            pool.wait_ge(s["pool_chain"], n)

            def front(b):
                if masked_ctx:
                    pool.wait_ge(s["var_ready"], b + 1)
                    pool.tensor_tensor(rstd[:], rstd[:], half[:], ALU.pow).then_inc(s["rstd_ready"], 1)
                    hold(pool, s["rstd_ready"], b + 1, s)
                    for i in range(4):
                        t = (x_in if i < 2 else c_in)[:, i % 2]
                        pool.tensor_scalar(t, t, mv[:, i, 0:1], rstd[:, i:i + 1], ALU.subtract, ALU.mult
                                           ).then_inc(s["x_ready"], 1)
                if cross:
                    pool.wait_ge(s["c_loaded"], IT * (b + 1))
                    hold(pool, s["x_seen"], b + 1, s)
                    for t in range(TT):
                        pool.tensor_scalar(c_in[:, t], c_in[:, t], m_next[:, t:t + 1], None, ALU.mult
                                           ).then_inc(s["c_masked"], 1)

            def turn(b, last=False):
                if not last:
                    front(b + 1)
                if masked_ctx:
                    pool.wait_ge(s["res_loaded"], IT * (b + 1))
                    for t in range(TT):
                        pool.tensor_tensor(res[:, t], res[:, t], p_bias[:], ALU.add).then_inc(s["res_biased"], 1)
                if causal or cross:
                    for i in range(2 if cross else 1):
                        n = 2 if cross else 1
                        pool.wait_ge(s["lnvar"], n * b + i + 1)
                        pool.tensor_tensor(rstd[:], rstd[:], half[:], ALU.pow).then_inc(s["lnrstd"], 1)

            if masked_ctx:
                pool.wait_ge(s["vec_loaded"], IT * NV)
            front(0)
            with pool.Fori(0, B - 1) as b:
                turn(b)
            turn(B - 1, last=True)

        @block.scalar
        def _(act):
            act.wait_ge(s["vec_loaded"], IT * NV)
            if masked_ctx:
                act.wait_ge(s["setup"], 1)
            for i in range(NM):
                act.wait_ge(s[f"stage_loaded{i % 2}"], IT * (i // 2 + 1))
                st = stage[:, i % 2]
                for k in range(KC):
                    if masked_ctx and i < 3:
                        sc = wq_scale[:, k:k + 1] if i == 0 else wcol[:, 2, k:k + 1]
                        ins = act.activation(W[0][:, i, k], st[:, k], ACT.Identity, scale=sc)
                    else:
                        ins = act.activation(W[0][:, i, k], st[:, k], ACT.Copy, scale=-SCALE if i == 0 else 1.0)
                ins.then_inc(s["w_hi_done"], 1)

            def turned(b, k):
                act.wait_ge(s["t_ps"], NP * b + k + 1)
                to = (xT if k < 2 else cT)[0][:, 2 * (k % 2):2 * (k % 2) + 2, :]
                act.activation(to, TB[k % 2][:].rearrange("p (c t) -> p c t", c=2), ACT.Copy
                               ).then_inc(s["t_hi"], 1)

            def qk(b, c):
                act.wait_ge(s["qk_ps"], KC * b + c + 1)
                if masked_ctx:
                    act.activation(K32[:], G[:, S:2 * S], ACT.Identity, bias=qk_bias[:, 1, c:c + 1])
                    ins = act.activation(Q[0][:, c % 2, :], G[:, 0:S], ACT.Identity, bias=qk_bias[:, 0, c:c + 1])
                else:
                    act.activation(K32[:], G[:, S:2 * S], ACT.Copy)
                    ins = act.activation(Q[0][:, c % 2, :], G[:, 0:S], ACT.Copy)
                ins.then_inc(s["qk_hi"], 1)

            def values(b, first=False):
                if not masked_ctx:
                    for t in range(TT):
                        act.wait_ge(s["v_ps"], TT * b + t + 1)
                        if not first:
                            act.wait_ge(s["av_done"], UNITS * b)
                        act.activation(V[:, t, :, 0:DH], SC[1 + t][:].rearrange("p (h d) -> p h d", h=H), ACT.Copy
                                       ).then_inc(s["v_ready"], 1)

            def width(u):
                return P if causal and (u // 2) % 2 == 0 else S

            def exps(b, u):
                act.wait_ge(s["masked"], UNITS * b + u + 1)
                w = width(u)
                for j in range(2):
                    ins = act.activation(prob[:, u % 3, j, 0:w], SC[u % 3][:, j * w:(j + 1) * w], ACT.Exp,
                                         bias=low[:, u % 3, j:j + 1], scale=-1.0)
                ins.then_inc(s["exp_done"], 1)

            def copy(b, u):
                act.wait_ge(s["pt_ready"], UNITS * b + u + 1)
                n = 2 * width(u)
                act.activation(probT[:, u % 3, 0:n], PT[u % 2][:, 0:n], ACT.Copy).then_inc(s["copied"], 1)

            def turn(b, last=False):
                for t in range(UNITS + 3):
                    if t >= 3:
                        copy(b, t - 3)
                    if t < UNITS:
                        exps(b, t)
                    if t % 4 == 1 and t // 4 < KC - 1:
                        qk(b, t // 4 + 1)
                    if not last and 13 <= t < 13 + NP:
                        turned(b + 1, t - 13)
                if not last:
                    qk(b + 1, 0)
                    values(b + 1)
                if masked_ctx:
                    for p in range(2):
                        act.wait_ge(s["post_ps"], 2 * b + p + 1)
                        act.activation(zT[0][:, 2 * p:2 * p + 2, :],
                                       SC[p][:].rearrange("p (c t) -> p c t", c=2), ACT.Copy
                                       ).then_inc(s["post_hi"], 1)
                if cross:
                    for p in range(2):
                        act.wait_ge(s["post_ps"], 2 * b + p + 1)
                        act.activation(x2T[0][:, 2 * p:2 * p + 2, :],
                                       SC[p][:].rearrange("p (c t) -> p c t", c=2), ACT.Copy
                                       ).then_inc(s["post_hi"], 1)
                    for p in range(2):
                        act.wait_ge(s["f1_ps"], 2 * b + p + 1)
                        for i in range(2):
                            m = 2 * p + i
                            ins = act.activation(h32[:, m, :], SC[2 - p][:, i * S:(i + 1) * S], ACT.Relu,
                                                 bias=f1b[:, m:m + 1])
                        ins.then_inc(s["f1_act"], 1)

            for k in range(NP):
                turned(0, k)
            act.wait_ge(s["setup"], 2)
            if masked_ctx:
                act.wait_ge(s["bias_done"], 3)
            qk(0, 0)
            values(0, first=True)
            with act.Fori(0, B - 1) as b:
                turn(b)
            turn(B - 1, last=True)

        @block.vector
        def _(dve):
            head = {"mask": 2, "causal": 5, "cross": 5}[kind]
            per = {"mask": 6, "causal": 27, "cross": 33}[kind]
            chain = Chain(dve, s["chain"], head, per)
            dve.wait_ge(s["vec_loaded"], IT * NV)
            if masked_ctx:
                dve.tensor_scalar(wq_scale[:], wcol[:, 0, :], -SCALE, None, ALU.mult).then_inc(s["setup"], 1)
            else:
                dve.sem_inc(s["setup"], 1)
            for part in range(2):
                dve.memset(K[part][:].bitcast(F32), 0.0)
            if masked_ctx:
                dve.memset(bias_rep[:], 1.0)
            else:
                dve.memset(ones[:], 1.0)
                dve.memset(big[:], BIG)
            dve.memset(V[:, :, :, DH:DH + 1], 1.0).then_inc(s["setup"], 1)
            dve.wait_ge(s["setup"], 2)
            if masked_ctx:
                for k in range(KC):
                    ins = dve.tensor_scalar(bias_rep[:, k, :], bias_rep[:, k, :], wcol[:, 3, k:k + 1], None, ALU.mult)
                ins.then_inc(s["setup"], 1)
            for i in range(NM):
                dve.wait_ge(s["w_hi_done"], i + 1)
                st = stage[:, i % 2]
                hi = W[0][:, i].bitcast(F32)
                for k in range(KC):
                    if masked_ctx and i < 3:
                        sc = wq_scale[:, k:k + 1] if i == 0 else wcol[:, 2, k:k + 1]
                    else:
                        sc = -SCALE if i == 0 else 1.0
                    ins = dve.scalar_tensor_tensor(out=W[1][:, i, k], in0=st[:, k], scalar=sc, in1=hi[:, k],
                                                   op0=ALU.mult, op1=ALU.subtract)
                ins.then_inc(s["w_lo_done"], 1)
                if masked_ctx and i < 3:
                    dve.wait_ge(s["bias_ps"], i + 1)
                    if i == 0:
                        dve.tensor_scalar(qk_bias[:, 0, :], G[:, 0:KC], -SCALE, None, ALU.mult
                                          ).then_inc(s["bias_done"], 1)
                    elif i == 1:
                        dve.tensor_copy(qk_bias[:, 1, :], G[:, 0:KC]).then_inc(s["bias_done"], 1)
                    else:
                        dve.tensor_copy(v_bias[:], O[:]).then_inc(s["bias_done"], 1)

            def front(b):
                if masked_ctx:
                    dve.wait_ge(s["x_loaded"], IT * (b + 1))
                    dve.wait_ge(s["c_loaded"], IT * (b + 1))
                    for i in range(4):
                        ins = dve.bn_stats(stats[:, i, :], (x_in if i < 2 else c_in)[:, i % 2])
                    chain.done(ins)
                    chain.hold(s)
                    for i in range(4):
                        ins = dve.bn_aggr(mv[:, i, :], stats[:, i, :])
                    chain.done(ins)
                    chain.wait()
                    dve.tensor_scalar(rstd[:], mv[:, :, 1], EPS, None, ALU.add).then_inc(s["var_ready"], 1)
                else:
                    dve.wait_ge(s["x_loaded"], IT * (b + 1))
                    chain.done(dve.tensor_reduce(big[:], x_in[:], AX_X, ALU.max, apply_absolute_value=True))
                    chain.wait()
                    dve.tensor_scalar(m_next[:], big[:], 0.0, None, ALU.not_equal).then_inc(s["x_seen"], 1)

            def turned(b, k):
                dve.wait_ge(s["t_hi"], NP * b + k + 1)
                dst_t = (xT if k < 2 else cT)
                sl = slice(2 * (k % 2), 2 * (k % 2) + 2)
                dve.tensor_tensor(dst_t[1][:, sl, :], TB[k % 2][:].rearrange("p (c t) -> p c t", c=2),
                                  dst_t[0][:, sl, :].bitcast(F32), ALU.subtract).then_inc(s["t_lo"], 1)

            def query0(b, c):
                dve.wait_ge(s["qk_hi"], KC * b + c + 1)
                dve.tensor_scalar(Q0[:], head_of[:], G[:, 0:1], None, ALU.mult).then_inc(s["e0_in"], 1)

            def keys_hi(b, c):
                r = c % 2
                dve.wait_ge(s["qk_hi"], KC * b + c + 1)
                for j in range(HC):
                    part = slice(j * DH, (j + 1) * DH)
                    ins = dve.tensor_copy(K[0][part, r, j, :], K32[part, :])
                ins.then_inc(s["k_hi"], 1)
                if masked_ctx:
                    dve.scalar_tensor_tensor(out=Q[1][:, r, :], in0=G[:, 0:S], scalar=qk_bias[:, 0, c:c + 1],
                                             in1=Q[0][:, r, :].bitcast(F32), op0=ALU.add, op1=ALU.subtract
                                             ).then_inc(s["q_lo"], 1)
                else:
                    dve.tensor_tensor(Q[1][:, r, :], G[:, 0:S], Q[0][:, r, :].bitcast(F32), ALU.subtract
                                      ).then_inc(s["q_lo"], 1)

            def keys_lo(b, c, heads=range(HC)):
                r = c % 2
                if heads[0] == 0:
                    dve.wait_ge(s["k_hi"], KC * b + c + 1)
                for j in heads:
                    part = slice(j * DH, (j + 1) * DH)
                    ins = dve.tensor_tensor(K[1][part, r, j, :], K32[part, :], K[0][part, r, j, :].bitcast(F32),
                                            ALU.subtract)
                if heads[-1] == HC - 1:
                    ins.then_inc(s["qk_lo"], 1)

            def nonzero(b, c):
                dve.wait_ge(s["e0_ps"], KC * b + c + 1)
                dve.tensor_scalar(flags[:].rearrange("p t h -> p (t h)"), M[:, 0:TT * HC], 0.0, None, ALU.not_equal
                                  ).then_inc(s["flags_done"], 1)

            def cuts(b, c):
                r = c % 2
                dve.wait_ge(s["len_ps"], KC * b + c + 1)
                dve.tensor_copy(lens[:], M[:, 16:16 + HC]).then_inc(s["len_read"], 1)
                dve.wait_ge(s["len_read"], KC * b + c + 1)
                chain.done(dve.reciprocal(rlen[:], lens[:]))
                chain.wait()
                dve.tensor_scalar(nan0[:, r, :], rlen[:], 0.0, None, ALU.mult)
                for j in range(HC):
                    ins = dve.tensor_scalar(cut[:, r, j, :], key[:], lens[:, j:j + 1], BIG, ALU.is_ge, ALU.mult)
                chain.done(ins)
                chain.wait()

            def values(b, first=False):
                if masked_ctx:
                    for t in range(TT):
                        dve.wait_ge(s["v_ps"], TT * b + t + 1)
                        if not first:
                            dve.wait_ge(s["av_done"], UNITS * b)
                        dve.tensor_tensor(V[:, t, :, 0:DH], SC[1 + t][:].rearrange("p (h d) -> p h d", h=H),
                                          v_bias[:].rearrange("p (h d) -> p h d", h=H), ALU.add
                                          ).then_inc(s["v_ready"], 1)

            def mask_floats(b):
                dve.wait_ge(s["m_loaded"], IT * (b + 1))
                dve.tensor_scalar(mask[:], m_in[:], F32_MAX, None, ALU.mult).then_inc(s["m_ready"], 1)

            def masks_and_minima(b, u):
                c, qt, pr = u // 4, (u // 2) % 2, u % 2
                if masked_ctx and u == 0:
                    dve.wait_ge(s["m_ready"], b + 1)
                hold(dve, s["s_ready"], UNITS * b + u + 1, s)
                for j in range(2):
                    if masked_ctx:
                        w, extra = S, mask[:, qt, :]
                    elif causal:
                        w = P if qt == 0 else S
                        extra = cut[:, c % 2, 2 * pr + j, (P if qt else 0):(3 * P if qt else P)]
                    else:
                        w, extra = S, cut[:, c % 2, 2 * pr + j, :]
                    sc = SC[u % 3][:, j * w:(j + 1) * w]
                    ins = dve.tensor_tensor_reduce(sc, sc, extra, 1.0, F32_MAX, ALU.add, ALU.min,
                                                   low[:, u % 3, j:j + 1])
                ins.then_inc(s["masked"], 1)

            def attended(b, c):
                dve.wait_ge(s["av_done"], UNITS * b + 4 * (c + 1))
                chain.done(dve.reciprocal(rs[:], Ov[:, :, :, DH]))
                chain.wait()
                if lengths:
                    for t in range(TT):
                        ins = dve.tensor_tensor(rs[:, t, :], rs[:, t, :], nan0[:, c % 2, :], ALU.add)
                    chain.done(ins)
                    chain.wait()
                    for t in range(TT):
                        ins = dve.tensor_scalar(rs[:, t, :], rs[:, t, :], m_cur[:, t:t + 1], None, ALU.mult)
                    chain.done(ins)
                    chain.wait()
                dve.tensor_tensor(z[:, :, c * P:(c + 1) * P].rearrange("p t (h d) -> p t h d", h=HC),
                                  Ov[:, :, :, 0:DH], rs[:].unsqueeze(3).to_broadcast([P, TT, HC, DH]), ALU.mult
                                  ).then_inc(s["z_done"], 1)

            def layer_norm(gain, shift, b, n, i):
                for t in range(TT):
                    ins = dve.bn_stats(stats[:, t, :], res[:, t])
                chain.done(ins)
                chain.hold(s)
                for t in range(TT):
                    ins = dve.bn_aggr(mv[:, t, :], stats[:, t, :])
                chain.done(ins)
                chain.wait()
                dve.tensor_scalar(rstd[:], mv[:, :, 1], EPS, None, ALU.add).then_inc(s["lnvar"], 1)
                for t in range(TT):
                    ins = dve.scalar_tensor_tensor(out=res[:, t], in0=res[:, t], scalar=mv[:, t, 0:1], in1=gain[:],
                                                   op0=ALU.subtract, op1=ALU.mult)
                chain.done(ins)
                chain.wait()
                dve.wait_ge(s["lnrstd"], n * b + i + 1)
                for t in range(TT):
                    ins = dve.scalar_tensor_tensor(out=res[:, t], in0=res[:, t], scalar=rstd[:, t:t + 1],
                                                   in1=shift[:], op0=ALU.mult, op1=ALU.add)
                return ins

            def post(b):
                if masked_ctx:
                    for p in range(2):
                        dve.wait_ge(s["post_hi"], 2 * b + p + 1)
                        dve.tensor_tensor(zT[1][:, 2 * p:2 * p + 2, :], SC[p][:].rearrange("p (c t) -> p c t", c=2),
                                          zT[0][:, 2 * p:2 * p + 2, :].bitcast(F32), ALU.subtract
                                          ).then_inc(s["post_lo"], 1)
                else:
                    dve.wait_ge(s["res_loaded"], IT * (b + 1))
                    dve.wait_ge(s["z_done"], KC * (b + 1) + 1)
                    for t in range(TT):
                        ins = dve.tensor_tensor(res[:, t], res[:, t], z[:, t], ALU.add)
                    chain.done(ins)
                    chain.wait()
                    ins = layer_norm(g_rep, b_rep, b, 2 if cross else 1, 0)
                    if causal:
                        ins.then_inc(s["out_ready"], 1)
                    else:
                        ins.then_inc(s["res_done"], 1)

            def project(b):
                for t in range(TT):
                    dve.wait_ge(s["proj_ps"], TT * b + t + 1)
                    if t == 0:
                        dve.wait_ge(s["res_biased"], TT * (b + 1))
                    ins = dve.tensor_tensor(res[:, t], PT[t][:], res[:, t], ALU.add)
                ins.then_inc(s["out_ready"], 1)

            def feed_forward(b):
                for p in range(2):
                    dve.wait_ge(s["post_hi"], 2 * b + p + 1)
                    dve.tensor_tensor(x2T[1][:, 2 * p:2 * p + 2, :], SC[p][:].rearrange("p (c t) -> p c t", c=2),
                                      x2T[0][:, 2 * p:2 * p + 2, :].bitcast(F32), ALU.subtract
                                      ).then_inc(s["post_lo"], 1)
                for p in range(2):
                    sl = slice(2 * p, 2 * p + 2)
                    dve.wait_ge(s["f1_act"], 2 * b + p + 1)
                    dve.tensor_copy(hT[0][:, sl, :], h32[:, sl, :]).then_inc(s["f1_hi"], 1)
                    dve.wait_ge(s["f1_hi"], 2 * b + p + 1)
                    dve.tensor_tensor(hT[1][:, sl, :], h32[:, sl, :], hT[0][:, sl, :].bitcast(F32), ALU.subtract
                                      ).then_inc(s["f1_lo"], 1)
                for t in range(TT):
                    dve.wait_ge(s["proj_ps"], TT * b + t + 1)
                    chain.done(dve.tensor_tensor(z[:, t], PT[t][:], f2b[:], ALU.add))
                chain.wait()
                for t in range(TT):
                    ins = dve.scalar_tensor_tensor(out=res[:, t], in0=z[:, t], scalar=m0[:, t:t + 1], in1=res[:, t],
                                                   op0=ALU.mult, op1=ALU.add)
                chain.done(ins)
                chain.wait()
                layer_norm(g3, b3, b, 2, 1).then_inc(s["out_ready"], 1)

            def rows_kept(b, nb):
                chain.done(dve.tensor_copy(m_cur[:], m_next[:]))
                if causal:
                    chain.done(dve.tensor_copy(keep[:, bass.ds(nb * TT, TT)], m_next[:]))
                if cross:
                    chain.done(dve.tensor_copy(m0[:], keep[:, bass.ds(nb * TT, TT)]))
                chain.wait()

            def turn(b, last=False):
                chain.turn(b)
                for t in range(UNITS + 2):
                    c, i = t // 4, t % 4
                    ahead = c + 1 < KC
                    if lengths and i == 0 and 1 <= c < KC:
                        cuts(b, c)
                    if lengths and i == 2 and ahead:
                        query0(b, c + 1)
                    if lengths and i == 3 and ahead:
                        nonzero(b, c + 1)
                    if i == 3 and ahead:
                        keys_lo(b, c + 1, (0, 1))
                    if not last and 14 <= t < 14 + NP:
                        turned(b + 1, t - 14)
                    if t < UNITS:
                        masks_and_minima(b, t)
                    if i == 2 and ahead:
                        keys_hi(b, c + 1)
                    if i == 3 and ahead:
                        keys_lo(b, c + 1, (2, 3))
                    if i == 3 and c >= 1:
                        attended(b, c - 1)
                    if not last and t == 5:
                        front(b + 1)
                if masked_ctx and not last:
                    mask_floats(b + 1)
                if not last:
                    if lengths:
                        query0(b + 1, 0)
                    keys_hi(b + 1, 0)
                    keys_lo(b + 1, 0)
                    if lengths:
                        nonzero(b + 1, 0)
                attended(b, KC - 1)
                if not last:
                    values(b + 1)
                post(b)
                if lengths and not last:
                    cuts(b + 1, 0)
                if masked_ctx:
                    project(b)
                if cross:
                    feed_forward(b)
                if lengths and not last:
                    rows_kept(b, b + 1)

            dve.sem_inc(s["z_done"], 1)
            front(0)
            for k in range(NP):
                turned(0, k)
            if masked_ctx:
                mask_floats(0)
            if lengths:
                dve.wait_ge(s["pool_setup"], 4 if causal else 3)
                query0(0, 0)
            keys_hi(0, 0)
            keys_lo(0, 0)
            values(0, first=True)
            if lengths:
                nonzero(0, 0)
                cuts(0, 0)
                rows_kept(0, 0)
            with dve.Fori(0, B - 1) as b:
                turn(b)
            turn(B - 1, last=True)

        @block.tensor
        def _(pe):
            pe.wait_ge(s["pool_setup"], 1)
            if masked_ctx:
                pe.wait_ge(s["vec_loaded"], IT * NV)
                pe.wait_ge(s["setup"], 3)
                for i in range(3):
                    pe.wait_ge(s[f"stage_loaded{i % 2}"], IT * (i // 2 + 1))
                    if i < 2:
                        if i:
                            pe.wait_ge(s["bias_done"], i)
                        for m in range(KC):
                            for k in range(KC):
                                ins = pe.matmul(G[:, m:m + 1], stage[:, i % 2, k, m * P:(m + 1) * P],
                                                wcol[:, 1 if i == 0 else 3, k:k + 1],
                                                start=(k == 0), stop=(k == KC - 1))
                    else:
                        for k in range(KC):
                            ins = pe.matmul(O[:], bias_rep[:, k, :], stage[:, i % 2, k, :],
                                            start=(k == 0), stop=(k == KC - 1))
                    ins.then_inc(s["bias_ps"], 1)

            def turn_over(b, k, first=False):
                src = x_in if k < 2 else c_in
                if k % 2 == 0:
                    if masked_ctx:
                        pe.wait_ge(s["x_ready"], 4 * b + k + 2)
                    elif k == 0:
                        pe.wait_ge(s["x_loaded"], IT * (b + 1))
                    else:
                        pe.wait_ge(s["c_masked"], TT * (b + 1))
                if k >= 2:
                    pe.wait_ge(s["t_lo"], NP * b + k - 1)
                if k == 1 and lengths and not first:
                    pe.wait_ge(s["len_read"], KC * b)
                for i in range(2):
                    ch = 2 * (k % 2) + i
                    for t in range(TT):
                        ins = pe.transpose(TB[k % 2][:, i * S + t * P:i * S + (t + 1) * P],
                                           src[:, t, ch * P:(ch + 1) * P], ident[:])
                ins.then_inc(s["t_ps"], 1)

            def values(b):
                for t in range(TT):
                    yield_value(b, t)

            def yield_value(b, t):
                if t == 0:
                    pe.wait_ge(s["t_lo"], NP * (b + 1))
                product(pe, SC[1 + t][:], lambda k, a: cT[a][:, k, t * P:(t + 1) * P],
                        lambda k, c: W[c][:, 2, k, :]).then_inc(s["v_ps"], 1)

            def queries(b, c):
                if c == 0:
                    pe.wait_ge(s["t_lo"], NP * b + 2 if two else NP * (b + 1))
                    if two:
                        pe.wait_ge(s["t_lo"], NP * b + 3)
                elif c >= 2:
                    pe.wait_ge(s["q_lo"], KC * b + c)
                product(pe, G[:, 0:S], lambda k, a: W[a][:, 0, k, c * P:(c + 1) * P], lambda k, p: xT[p][:, k, :])

            def keys(b, c):
                if c == 0:
                    pe.wait_ge(s["t_lo"], NP * (b + 1))
                product(pe, G[:, S:2 * S], lambda k, a: W[a][:, 1, k, c * P:(c + 1) * P],
                        lambda k, p: cT[p][:, k, :]).then_inc(s["qk_ps"], 1)

            def energies0(b, c):
                pe.wait_ge(s["e0_in"], KC * b + c + 1)
                for kt in range(TT):
                    ins = pe.matmul(M[:, kt * HC:(kt + 1) * HC], K32[:, kt * P:(kt + 1) * P], Q0[:],
                                    start=True, stop=True)
                ins.then_inc(s["e0_ps"], 1)

            def count(b, c):
                pe.wait_ge(s["flags_done"], KC * b + c + 1)
                for kt in range(TT):
                    ins = pe.matmul(M[:, 16:16 + HC], ones[:], flags[:, kt, :], start=(kt == 0), stop=(kt == TT - 1))
                ins.then_inc(s["len_ps"], 1)

            def scores(b, u):
                c, qt, pr = u // 4, (u // 2) % 2, u % 2
                w = P if causal and qt == 0 else S
                if u % 4 == 0:
                    pe.wait_ge(s["qk_lo"], KC * b + c + 1)
                if u == 2:
                    pe.wait_ge(s["v_ready"], TT * (b + 1))
                if u == 1:
                    pe.wait_ge(s["v_ready"], TT * (b + 1) - 1)
                n = 0
                for a, k in PASSES:
                    ins = pe.matmul(SC[u % 3][:, 0:2 * w].rearrange("p (h k) -> p h k", h=2),
                                    Q[a][:, c % 2, qt * P:(qt + 1) * P], K[k][:, c % 2, 2 * pr:2 * pr + 2, 0:w],
                                    start=(n == 0), stop=(n == 2))
                    n += 1
                ins.then_inc(s["s_ready"], 1)

            def turn_probs(b, u):
                w = P if causal and (u // 2) % 2 == 0 else S
                pe.wait_ge(s["exp_done"], UNITS * b + u + 1)
                if u >= 2:
                    pe.wait_ge(s["copied"], UNITS * b + u - 1)
                n = 0
                for j in range(2):
                    for kt in range(w // P):
                        ins = pe.transpose(PT[u % 2][:, n * P:(n + 1) * P], prob[:, u % 3, j, kt * P:(kt + 1) * P],
                                           ident[:])
                        n += 1
                ins.then_inc(s["pt_ready"], 1)

            def attend(b, u):
                c, qt, pr = u // 4, (u // 2) % 2, u % 2
                nk = 1 if causal and qt == 0 else TT
                pe.wait_ge(s["copied"], UNITS * b + u + 1)
                if u % 4 == 0:
                    pe.wait_ge(s["z_done"], KC * b + c + 1)
                for j in range(2):
                    hh = 2 * pr + j
                    for kt in range(nk):
                        ins = pe.matmul(Ov[:, qt, hh, :], probT[:, u % 3, (j * nk + kt) * P:(j * nk + kt + 1) * P],
                                        V[:, kt, HC * c + hh, :], start=(kt == 0), stop=(kt == nk - 1))
                ins.then_inc(s["av_done"], 1)

            def turn(b, last=False):
                for t in range(UNITS + 4):
                    c, i = t // 4, t % 4
                    if t < UNITS:
                        scores(b, t)
                    if 2 <= t < UNITS + 2:
                        turn_probs(b, t - 2)
                    if t >= 4:
                        attend(b, t - 4)
                    if t == 0:
                        queries(b, 1)
                    if i == 3 and c + 2 < KC:
                        queries(b, c + 2)
                    if i == 0 and c + 1 < KC:
                        keys(b, c + 1)
                    if lengths and i == 2 and c + 1 < KC:
                        energies0(b, c + 1)
                    if lengths and i == 3 and c + 1 < KC:
                        count(b, c + 1)
                    if not last:
                        if 12 <= t < 12 + NP:
                            turn_over(b + 1, t - 12)
                        if t == UNITS:
                            queries(b + 1, 0)
                        if t == UNITS + 1:
                            keys(b + 1, 0)
                        if t == UNITS + 2:
                            yield_value(b + 1, 0)
                        if t == UNITS + 3:
                            if lengths:
                                energies0(b + 1, 0)
                                count(b + 1, 0)
                            yield_value(b + 1, 1)
                if masked_ctx:
                    pe.wait_ge(s["z_done"], KC * (b + 1) + 1)
                    src, dst_t = z, zT
                elif cross:
                    pe.wait_ge(s["res_done"], b + 1)
                    src, dst_t = res, x2T
                if masked_ctx or cross:
                    for p in range(2):
                        if p == 1 and not last:
                            pe.wait_ge(s["v_ready"], TT * (b + 2) - 1)
                        for i in range(2):
                            for t in range(TT):
                                ch = 2 * p + i
                                ins = pe.transpose(SC[p][:, i * S + t * P:i * S + (t + 1) * P],
                                                   src[:, t, ch * P:(ch + 1) * P], ident[:])
                        ins.then_inc(s["post_ps"], 1)
                    pe.wait_ge(s["post_lo"], 2 * (b + 1))
                if masked_ctx:
                    for t in range(TT):
                        product(pe, PT[t][:], lambda k, a: zT[a][:, k, t * P:(t + 1) * P],
                                lambda k, p: W[p][:, 3, k, :]).then_inc(s["proj_ps"], 1)
                if cross:
                    for p in range(2):
                        if p == 0 and not last:
                            pe.wait_ge(s["v_ready"], TT * (b + 2))
                        for i in range(2):
                            m = 2 * p + i
                            ins = product(pe, SC[2 - p][:, i * S:(i + 1) * S],
                                          lambda k, a: W[a][:, 3, k, m * P:(m + 1) * P], lambda k, q: x2T[q][:, k, :])
                        ins.then_inc(s["f1_ps"], 1)
                    pe.wait_ge(s["f1_lo"], 2 * (b + 1))
                    for t in range(TT):
                        product(pe, PT[t][:], lambda k, a: hT[a][:, k, t * P:(t + 1) * P],
                                lambda k, p: W[p][:, 4, k, :]).then_inc(s["proj_ps"], 1)

            for k in range(NP):
                turn_over(0, k, first=True)
            pe.wait_ge(s["w_lo_done"], NM)
            if masked_ctx:
                pe.wait_ge(s["bias_done"], 3)
            queries(0, 0)
            keys(0, 0)
            values(0)
            if lengths:
                pe.wait_ge(s["setup"], 2)
                energies0(0, 0)
                count(0, 0)
            with pe.Fori(0, B - 1) as b:
                turn(b)
            turn(B - 1, last=True)


def mlp_phase(nc, x_src, dst, w1, w2, n_w, n_b, b1, b2):
    NT = 4
    N = NT * P
    TURNS = B * S // N
    MH = HID // P
    x_t = x_src.rearrange("b s c -> (b s) c").rearrange("(n t p) c -> n p t c", t=NT, p=P)
    d_t = dst.rearrange("b s c -> (b s) c").rearrange("(n t p) c -> n p t c", t=NT, p=P)
    with ExitStack() as ctx:
        def sb(name, shape, dt=F32):
            return ctx.enter_context(nc.sbuf_tensor(f"mlp_{name}", shape, dt))

        def bank(name):
            return ctx.enter_context(nc.psum_tensor(f"mlp_{name}", [P, 512], F32))

        W1 = [sb(f"w1_{part}", [P, KC, HID], F32R) for part in ("hi", "lo")]
        W2 = [sb(f"w2_{part}", [P, MH, C], F32R) for part in ("hi", "lo")]
        x = sb("x", [P, NT, C])
        xn = sb("xn", [P, NT, C])
        xT = [sb(f"xT_{part}", [P, KC, N], F32R) for part in ("hi", "lo")]
        h32 = sb("h32", [P, 2, N])
        hT = [sb(f"hT_{part}", [P, 2, N], F32R) for part in ("hi", "lo")]
        y = sb("y", [P, NT, C])
        ident = sb("ident", [P, P])
        ncol = sb("ncol", [P, 2, KC])
        b1col = sb("b1col", [P, MH])
        hb = sb("hb", [P, MH])
        b2r = sb("b2r", [P, C])
        stats = sb("stats", [P, NT, 6])
        mv = sb("mv", [P, NT, 2])
        rstd = sb("rstd", [P, NT])
        half = sb("half", [P, NT])
        ACC = [bank(f"acc{i}") for i in range(NT)]
        F1 = [bank(f"f1_{i}") for i in range(2)]
        TB = [bank(f"turned{i}") for i in range(2)]
        s = Signals(nc, "mlp")
        ctx.callback(s.close)
        pieces = [(w1.rearrange("(k p) n -> p k n", p=P)[:, :, 512 * i:512 * (i + 1)]) for i in range(4)]
        pieces += [(w2.rearrange("(k p) n -> p k n", p=P)[:, 4 * i:4 * i + 4, :]) for i in range(4)]
        stages = [xn, y]

        def part_of(w, i):
            return W1[w][:, :, 512 * i:512 * (i + 1)] if i < 4 else W2[w][:, 4 * (i - 4):4 * (i - 4) + 4, :]

        block = ctx.enter_context(nc.Block())

        @block.sync
        def _(sp):
            for to, frm in ((ncol[:, 0, :], (n_w)), (ncol[:, 1, :], (n_b)), (b1col[:], (b1)),
                            (b2r[:], b2.partition_broadcast(P))):
                sp.dma_start(to, frm).then_inc(s["vec_loaded"], IT)
            sp.dma_start(x[:], x_t[0]).then_inc(s["x_loaded"], IT)
            for i, piece in enumerate(pieces):
                if i >= 2:
                    sp.wait_ge(s["w_lo"], i - 1)
                    if i - 2 < 4:
                        sp.wait_ge(s["bias_ps"], i - 1)
                sp.dma_start(stages[i % 2][:], piece).then_inc(s[f"stage_loaded{i % 2}"], IT)

            def turn(b, last=False):
                if not last:
                    hold(sp, s["xn_ready"], NT * (b + 1), s)
                    hold(sp, s["x_biased"], NT * (b + 1), s)
                    sp.dma_start(x[:], x_t[bass.ds(b + 1, 1)].rearrange("o p t c -> p (o t) c")
                                 ).then_inc(s["x_loaded"], IT)
                hold(sp, s["out_ready"], b + 1, s)
                sp.dma_start(d_t[bass.ds(b, 1)].rearrange("o p t c -> p (o t) c"), y[:]).then_inc(s["stored"], IT)
                hold(sp, s["stored"], IT * (b + 1), s)

            with sp.Fori(0, TURNS - 1) as b:
                turn(b)
            turn(TURNS - 1, last=True)

        @block.gpsimd
        def _(pool):
            pool.memset(ident[:], 0.0).then_inc(s["pool_chain"], 1)
            pool.memset(half[:], -0.5).then_inc(s["pool_chain"], 1)
            pool.wait_ge(s["pool_chain"], 2)
            pool.affine_select(out=ident[:], in_=ident[:], compare_op=ALU.not_equal, fill=1.0, base=0,
                               pattern=[[-1, P]], channel_multiplier=1).then_inc(s["pool_setup"], 1)

            def power(b):
                pool.wait_ge(s["var_ready"], b + 1)
                pool.tensor_tensor(rstd[:], rstd[:], half[:], ALU.pow).then_inc(s["rstd_ready"], 1)

            def residual(b, first=False):
                if not first:
                    pool.wait_ge(s["stored"], IT * b)
                for t in range(NT):
                    pool.tensor_tensor(y[:, t], x[:, t], b2r[:], ALU.add).then_inc(s["x_biased"], 1)

            pool.wait_ge(s["vec_loaded"], 4 * IT)
            power(0)
            pool.wait_ge(s["w_lo"], 8)
            residual(0, first=True)
            with pool.Fori(0, TURNS - 1) as b:
                power(b + 1)
                residual(b + 1)

        @block.scalar
        def _(act):
            act.wait_ge(s["vec_loaded"], 4 * IT)
            for i in range(8):
                act.wait_ge(s[f"stage_loaded{i % 2}"], IT * (i // 2 + 1))
                for k in range(4):
                    src = stages[i % 2][:, k, :]
                    dst_w = part_of(0, i)[:, k, :]
                    if i < 4:
                        ins = act.activation(dst_w, src, ACT.Identity, scale=ncol[:, 0, k:k + 1])
                    else:
                        ins = act.activation(dst_w, src, ACT.Copy)
                ins.then_inc(s["w_hi"], 1)

            def turned(b, k):
                act.wait_ge(s["t_ps"], KC * b + k + 1)
                act.activation(xT[0][:, k, :], TB[k % 2][:], ACT.Copy).then_inc(s["t_hi"], 1)

            def gelu(b, m):
                act.wait_ge(s["f1_ps"], MH * b + m + 1)
                act.activation(h32[:, m % 2, :], F1[m % 2][:], ACT.Gelu, bias=hb[:, m:m + 1]).then_inc(s["gelu"], 1)

            for k in range(KC):
                turned(0, k)
            act.wait_ge(s["bias_done"], 1)
            with act.Fori(0, TURNS - 1) as b:
                for m in range(MH):
                    gelu(b, m)
                for k in range(KC):
                    turned(b + 1, k)
            for m in range(MH):
                gelu(TURNS - 1, m)

        @block.vector
        def _(dve):
            dve.sem_inc(s["acc_read"], 1)

            def norm(b):
                dve.wait_ge(s["x_loaded"], IT * (b + 1))
                for t in range(NT):
                    ins = dve.bn_stats(stats[:, t, :], x[:, t])
                ins.then_inc(s["stats_done"], 1)
                hold(dve, s["stats_done"], b + 1, s)
                for t in range(NT):
                    ins = dve.bn_aggr(mv[:, t, :], stats[:, t, :])
                ins.then_inc(s["mv_done"], 1)
                dve.wait_ge(s["mv_done"], b + 1)
                dve.tensor_scalar(rstd[:], mv[:, :, 1], EPS, None, ALU.add).then_inc(s["var_ready"], 1)

            def apply(b):
                dve.wait_ge(s["rstd_ready"], b + 1)
                for t in range(NT):
                    dve.tensor_scalar(xn[:, t], x[:, t], mv[:, t, 0:1], rstd[:, t:t + 1], ALU.subtract, ALU.mult
                                      ).then_inc(s["xn_ready"], 1)

            def turned(b, k):
                dve.wait_ge(s["t_hi"], KC * b + k + 1)
                dve.tensor_tensor(xT[1][:, k, :], TB[k % 2][:], xT[0][:, k, :].bitcast(F32), ALU.subtract
                                  ).then_inc(s["t_lo"], 1)

            def split(b, m):
                r = m % 2
                dve.wait_ge(s["gelu"], MH * b + m + 1)
                dve.tensor_copy(hT[0][:, r, :], h32[:, r, :]).then_inc(s["h_hi"], 1)
                dve.wait_ge(s["h_hi"], MH * b + m + 1)
                dve.tensor_tensor(hT[1][:, r, :], h32[:, r, :], hT[0][:, r, :].bitcast(F32), ALU.subtract
                                  ).then_inc(s["h_lo"], 1)

            def finish(b):
                dve.wait_ge(s["x_biased"], NT * (b + 1))
                for t in range(NT):
                    dve.wait_ge(s["acc_ready"], NT * b + t + 1)
                    ins = dve.tensor_tensor(y[:, t], ACC[t][:], y[:, t], ALU.add)
                    ins.then_inc(s["acc_read"], 1)
                dve.wait_ge(s["acc_read"], NT * (b + 1) + 1)
                dve.sem_inc(s["out_ready"], 1)

            norm(0)
            for i in range(8):
                dve.wait_ge(s["w_hi"], i + 1)
                for k in range(4):
                    src = stages[i % 2][:, k, :]
                    hi = part_of(0, i)[:, k, :].bitcast(F32)
                    if i < 4:
                        ins = dve.scalar_tensor_tensor(out=part_of(1, i)[:, k, :], in0=src, scalar=ncol[:, 0, k:k + 1],
                                                       in1=hi, op0=ALU.mult, op1=ALU.subtract)
                    else:
                        ins = dve.tensor_tensor(part_of(1, i)[:, k, :], src, hi, ALU.subtract)
                ins.then_inc(s["w_lo"], 1)
            dve.wait_ge(s["bias_ps"], 4)
            dve.tensor_tensor(hb[:], F1[0][:, 0:MH], b1col[:], ALU.add).then_inc(s["bias_done"], 1)
            dve.wait_ge(s["w_lo"], 8)
            apply(0)
            for k in range(KC):
                turned(0, k)
            with dve.Fori(0, TURNS - 1) as b:
                for m in range(MH):
                    split(b, m)
                    if m == 8:
                        norm(b + 1)
                    if m == 10:
                        apply(b + 1)
                for k in range(KC):
                    turned(b + 1, k)
                finish(b)
            for m in range(MH):
                split(TURNS - 1, m)
            finish(TURNS - 1)

        @block.tensor
        def _(pe):
            pe.wait_ge(s["vec_loaded"], 4 * IT)
            for i in range(4):
                pe.wait_ge(s[f"stage_loaded{i % 2}"], IT * (i // 2 + 1))
                for j in range(4):
                    m = 4 * i + j
                    for k in range(KC):
                        ins = pe.matmul(F1[0][:, m:m + 1], stages[i % 2][:, k, j * P:(j + 1) * P], ncol[:, 1, k:k + 1],
                                        start=(k == 0), stop=(k == KC - 1))
                ins.then_inc(s["bias_ps"], 1)
            pe.wait_ge(s["pool_setup"], 1)

            def turn_over(b, k, first=False):
                if k == 0:
                    pe.wait_ge(s["xn_ready"], NT * (b + 1))
                if k >= 2:
                    pe.wait_ge(s["t_lo"], KC * b + k - 1)
                for t in range(NT):
                    ins = pe.transpose(TB[k % 2][:, t * P:(t + 1) * P], xn[:, t, k * P:(k + 1) * P], ident[:])
                ins.then_inc(s["t_ps"], 1)

            def hidden(b, m):
                product(pe, F1[m % 2][:], lambda k, a: W1[a][:, k, m * P:(m + 1) * P],
                        lambda k, p: xT[p][:, k, :]).then_inc(s["f1_ps"], 1)

            def down(b, m):
                pe.wait_ge(s["h_lo"], MH * b + m + 1)
                for t in range(NT):
                    if m == 0:
                        pe.wait_ge(s["acc_read"], NT * b + t + 1 if t == 0 else NT * b + 1)
                    for n, (a, p) in enumerate(PASSES):
                        ins = pe.matmul(ACC[t][:], hT[a][:, m % 2, t * P:(t + 1) * P], W2[p][:, m, :],
                                        start=(m == 0 and n == 0), stop=(m == MH - 1 and n == 2))
                    if m == MH - 1:
                        ins.then_inc(s["acc_ready"], 1)
                    elif t == NT - 1:
                        ins.then_inc(s["f2_step"], 1)

            def turn(b, last=False):
                for m in range(1, MH):
                    hidden(b, m)
                    down(b, m - 1)
                if not last:
                    for k in range(KC):
                        turn_over(b + 1, k)
                down(b, MH - 1)
                if not last:
                    pe.wait_ge(s["t_lo"], KC * (b + 2))
                    hidden(b + 1, 0)

            for k in range(KC):
                turn_over(0, k)
            pe.wait_ge(s["w_lo"], 8)
            pe.wait_ge(s["bias_done"], 1)
            pe.wait_ge(s["t_lo"], KC)
            hidden(0, 0)
            with pe.Fori(0, TURNS - 1) as b:
                turn(b)
            turn(TURNS - 1, last=True)


def two_layers(nc, a, out):
    x1 = nc.dram_tensor("after_attention0", [B, S, C], F32).ap()
    x2 = nc.dram_tensor("after_layer0", [B, S, C], F32).ap()
    x3 = nc.dram_tensor("after_attention1", [B, S, C], F32).ap()
    kv = a["L0_xattn_kv_w"]
    with nc.sbuf_tensor("rows_that_count", [P, B * TT], F32) as keep:
        attention_phase(nc, "mask", a["x"], a["ctx_1024"], a["mask_BxSxS2_bk0"], x1,
                        [a["L0_xattn_q_w"], kv[:, 0:C], kv[:, C:2 * C], a["L0_xattn_proj_w"]],
                        [a["L0_xattn_qn_w"], a["L0_xattn_qn_b"], a["L0_xattn_cn_w"], a["L0_xattn_cn_b"],
                         a["L0_xattn_proj_b"]], keep)
        mlp_phase(nc, x1, x2, a["L0_xattn_fc1_w"], a["L0_xattn_fc2_w"], a["L0_xattn_n2_w"], a["L0_xattn_n2_b"],
                  a["L0_xattn_fc1_b"], a["L0_xattn_fc2_b"])
        attention_phase(nc, "causal", x2, None, None, x3,
                        [a["L1_xattn_Wq1"], a["L1_xattn_Wk1"], a["L1_xattn_Wv1"]],
                        [a["L1_xattn_ln1_g"], a["L1_xattn_ln1_b"]], keep)
        attention_phase(nc, "cross", x3, a["ctx_1024"], None, out,
                        [a["L1_xattn_Wq2"], a["L1_xattn_Wk2"], a["L1_xattn_Wv2"], a["L1_xattn_fc1_w"],
                         a["L1_xattn_fc2_w"]],
                        [a["L1_xattn_ln2_g"], a["L1_xattn_ln2_b"], a["L1_xattn_fc1_b"], a["L1_xattn_fc2_b"],
                         a["L1_xattn_ln3_g"], a["L1_xattn_ln3_b"]], keep)


COLUMNS = ("L0_xattn_qn_w", "L0_xattn_qn_b", "L0_xattn_cn_w", "L0_xattn_cn_b", "L0_xattn_n2_w", "L0_xattn_n2_b",
           "L0_xattn_fc1_b", "L1_xattn_fc1_b")


def laid_out(name, a):
    a = np.asarray(a)
    if name.startswith("mask"):
        return np.ascontiguousarray(a)
    if "_Wq" in name or "_Wk" in name or "_Wv" in name:
        return np.ascontiguousarray(a.transpose(1, 0, 2)).reshape(C, C)
    if name in ("L1_xattn_fc1_w", "L1_xattn_fc2_w"):
        return np.ascontiguousarray(a.T)
    if name in COLUMNS:
        return np.ascontiguousarray(a.reshape(-1, P).T)
    return np.ascontiguousarray(a)


def kernel(**inputs):
    import concourse.bacc as _bacc
    from concourse.bass_utils import run_bass_kernel_spmd as _run

    nc = _bacc.Bacc("TRN2", target_bir_lowering=False, num_devices=1)
    arrays, args = {}, {}
    for name, value in inputs.items():
        v = laid_out(name, value)
        arrays[f"in_{name}"] = v
        args[name] = nc.dram_tensor(f"in_{name}", v.shape, mybir.dt.from_np(v.dtype), kind="ExternalInput").ap()
    out = nc.dram_tensor("out", [B, S, C], F32, kind="ExternalOutput").ap()
    two_layers(nc, args, out)
    r = _run(nc, [arrays], core_ids=[0])
    return r.results[0]["out"]
```

```python
from contextlib import ExitStack

import numpy as np

import concourse.bass as bass
from concourse import mybir

F32 = mybir.dt.float32
F32R = mybir.dt.float32r
BF16 = mybir.dt.bfloat16
I32 = mybir.dt.int32
U8 = mybir.dt.uint8
ALU = mybir.AluOpType
ACT = mybir.ActivationFunctionType
AX_X = mybir.AxisListType.X

P = 128
B, S, C = 16, 256, 512
H = 16
DH = C // H
KC = C // P
HC = P // DH
TT = S // P
HID = 4 * C
EPS = 1e-5
SCALE = float(DH) ** -0.5
F32_MAX = float(np.finfo(np.float32).max)
BIG = 3e38
BEYOND = 60000.0
UNITS = KC * TT * 2
IT = 16


class Chain:

    def __init__(self, eng, sem, head, per):
        self.eng, self.sem, self.head, self.per = eng, sem, head, per
        self.base, self.k, self.entered = 0, 0, False

    def turn(self, b):
        want = self.per if self.entered else self.head
        assert self.k == want, (self.sem, "steps", self.k, "of", want)
        self.entered = True
        self.base, self.k = self.head + (b - 1) * self.per, 0

    def done(self, ins):
        ins.then_inc(self.sem, 1)
        self.k += 1

    def wait(self):
        self.eng.wait_ge(self.sem, self.base + self.k)

    def hold(self, s):
        hold(self.eng, self.sem, self.base + self.k, s)


def rows(m):
    return m.rearrange("(k p) n -> p k n", p=P)


def tokens(t, b):
    return t[bass.ds(b, 1)].rearrange("o (t p) c -> p (o t) c", p=P)


def hold(eng, sem, value, s):
    eng.wait_ge(sem, value)
    eng.sem_inc(s["held"], 1)


class Signals(dict):

    def __init__(self, nc, phase):
        super().__init__()
        self.nc, self.phase = nc, phase

    def __missing__(self, name):
        self[name] = self.nc.alloc_semaphore(f"{self.phase}_{name}")
        return self[name]

    def close(self):
        self.nc.clear_and_free_semaphores(list(self.values()))
        self.nc.all_engine_barrier()


PASSES = ((0, 0), (0, 1), (1, 0))


def product(pe, out, lhs, rhs):
    last = None
    n = 0
    for k in range(KC):
        for a, c in PASSES:
            last = pe.matmul(out, lhs(k, a), rhs(k, c), start=(n == 0), stop=(n == KC * len(PASSES) - 1))
            n += 1
    return last


def attention_phase(nc, kind, x_src, ctx_src, mask_src, dst, mats, vecs, keep):
    masked_ctx, causal, cross = kind == "mask", kind == "causal", kind == "cross"
    lengths = not masked_ctx
    two = not causal
    NP = 4 if two else 2
    NM = len(mats)

    with ExitStack() as ctx:
        def sb(name, shape, dt=F32):
            return ctx.enter_context(nc.sbuf_tensor(f"{kind}_{name}", shape, dt))

        def bank(name, dt=F32):
            return ctx.enter_context(nc.psum_tensor(f"{kind}_{name}", [P, 512], dt))

        W = [sb(f"w_{part}", [P, NM, KC, C], F32R) for part in ("hi", "lo")]
        stage = sb("stage", [P, 2, KC, C])
        ident = sb("ident", [P, P])
        x_in = sb("x_in", [P, TT, C])
        res = sb("res", [P, TT, C])
        z = sb("z", [P, TT, C])
        xT = [sb(f"xT_{part}", [P, KC, S], F32R) for part in ("hi", "lo")]
        if two:
            c_in = sb("c_in", [P, TT, C])
            cT = [sb(f"cT_{part}", [P, KC, S], F32R) for part in ("hi", "lo")]
        else:
            cT = xT
        Q = [sb(f"q_{part}", [P, 2, S], F32R) for part in ("hi", "lo")]
        K = [sb(f"k_{part}", [P, 2, HC, S], F32R) for part in ("hi", "lo")]
        K32 = sb("k32", [P, S])
        V = sb("v", [P, TT, H, DH])
        OT = sb("ot", [P, S])
        sums = sb("sums", [P, KC, TT, HC])
        prob = sb("prob", [P, 2, 2, S])
        probT = sb("probT", [P, 4, 512])
        low = sb("low", [P, 4, 2])
        rs = sb("rs", [P, TT, HC])
        if masked_ctx:
            m_in = sb("m_in", [P, TT, S], U8)
            mask = sb("mask", [P, TT, S])
            wcol = sb("wcol", [P, 4, KC])
            wq_scale = sb("wq_scale", [P, KC])
            bias_rep = sb("bias_rep", [P, KC, P])
            qk_bias = sb("qk_bias", [P, 2, KC])
            v_bias = sb("v_bias", [P, C])
            p_bias = sb("p_bias", [P, C])
            stats = sb("stats", [P, 4, 6])
            mv = sb("mv", [P, 4, 2])
            rstd = sb("rstd", [P, 4])
            half = sb("half", [P, 4])
            zT = [sb(f"zT_{part}", [P, KC, S], F32R) for part in ("hi", "lo")]
        else:
            ones = sb("ones", [P, P], BF16)
            iota_i = sb("iota_i", [P, 3 * P if causal else S], I32)
            key = sb("key", [P, 3 * P if causal else S], BF16)
            head_of = sb("head_of", [P, HC])
            Q0 = sb("q0", [P, HC])
            flags = sb("flags", [P, TT, HC], BF16)
            lens = sb("lens", [P, HC])
            rlen = sb("rlen", [P, HC])
            nan0 = sb("nan0", [P, KC, HC])
            cut = sb("cut", [P, 2, HC, 3 * P if causal else S], BF16)
            big = sb("big", [P, TT])
            m_next = sb("m_next", [P, TT])
            m_cur = sb("m_cur", [P, TT])
            minus_mean = sb("minus_mean", [P, TT])
            offset = sb("offset", [P, TT])
            g_rep = sb("g_rep", [P, C])
            b_rep = sb("b_rep", [P, C])
            stats = sb("stats", [P, TT, 6])
            mv = sb("mv", [P, TT, 2])
            rstd = sb("rstd", [P, TT])
            half = sb("half", [P, TT])
        if cross:
            x2T = [sb(f"x2T_{part}", [P, KC, S], F32R) for part in ("hi", "lo")]
            h32 = sb("h32", [P, KC, S])
            hT = [sb(f"hT_{part}", [P, KC, S], F32R) for part in ("hi", "lo")]
            f1b = sb("f1b", [P, KC])
            f2b = sb("f2b", [P, C])
            g3 = sb("g3", [P, C])
            b3 = sb("b3", [P, C])
            m0 = sb("m0", [P, TT])

        SC = [bank(f"scores{i}") for i in range(2)]
        NPT = 1 if lengths else 2
        PT = [bank(f"probsT{i}") for i in range(NPT)]
        O = bank("attended")
        G = bank("qk")
        M = bank("lengths") if lengths else None
        X = [bank(f"work{i}") for i in range(2)]
        T_BANK = {"mask": (0, 1, 0, 1), "causal": (1, 0), "cross": (0, 0, 0, 1)}[kind]
        VA_BANK = {"mask": 1, "causal": 1, "cross": 0}[kind]
        VB_BANK = 0
        HALF = C // 2
        Oz = O[:, S:2 * S].rearrange("p (t h d) -> p t h d", t=TT, h=HC)
        PAIRS = UNITS // 2

        s = Signals(nc, kind)
        ctx.callback(s.close)

        def where_vecs():
            if masked_ctx:
                return [(wcol[:, i, :], v) for i, v in enumerate(vecs[0:4])] + [
                    (p_bias[:], vecs[4].partition_broadcast(P))]
            out = [(g_rep[:], vecs[0].partition_broadcast(P)), (b_rep[:], vecs[1].partition_broadcast(P))]
            if cross:
                out += [(f1b[:], vecs[2]), (f2b[:], vecs[3].partition_broadcast(P)),
                        (g3[:], vecs[4].partition_broadcast(P)), (b3[:], vecs[5].partition_broadcast(P))]
            return out

        NV = len(where_vecs())
        block = ctx.enter_context(nc.Block())

        @block.sync
        def _(sp):
            if masked_ctx:
                for to, frm in where_vecs():
                    sp.dma_start(to, frm).then_inc(s["vec_loaded"], IT)

            def load_inputs(b, first=False):
                if not first:
                    hold(sp, s["t_ps"], NP * b, s)
                    if lengths:
                        hold(sp, s["x_seen"], b, s)
                sp.dma_start(x_in[:], tokens(x_src, b)).then_inc(s["x_loaded"], IT)
                if two:
                    sp.dma_start(c_in[:], tokens(ctx_src, b)).then_inc(s["c_loaded"], IT)
                if masked_ctx:
                    if not first:
                        hold(sp, s["m_ready"], b, s)
                    sp.dma_start(m_in[:], mask_src[bass.ds(b, 1)].rearrange("o (t p) k -> p (o t) k", p=P)
                                 ).then_inc(s["m_loaded"], IT)

            load_inputs(0, first=True)
            for i, m in enumerate(mats):
                if i >= 2:
                    sp.wait_ge(s["w_hi_done"], i - 1)
                    sp.wait_ge(s["w_lo_done"], i - 1)
                    if masked_ctx and i - 2 < 3:
                        sp.wait_ge(s["bias_ps"], i - 1)
                sp.dma_start(stage[:, i % 2], rows(m)).then_inc(s[f"stage_loaded{i % 2}"], IT)
            if lengths:
                for to, frm in where_vecs():
                    sp.dma_start(to, frm).then_inc(s["vec_loaded"], IT)

            def turn(b, prev=True, nxt=True):
                if nxt:
                    load_inputs(b + 1)
                if prev:
                    hold(sp, s["stored"], IT * (b - 1) + 1, s)
                    sp.dma_start(res[:], tokens(x_src, b - 1)).then_inc(s["res_loaded"], IT)
                    hold(sp, s["out_ready"], b, s)
                    sp.dma_start(tokens(dst, b - 1), res[:]).then_inc(s["stored"], IT)

            sp.sem_inc(s["stored"], 1)
            turn(0, prev=False)
            with sp.Fori(1, B - 1) as b:
                turn(b)
            turn(B - 1, nxt=False)
            turn(B, nxt=False)
            sp.wait_ge(s["stored"], IT * B + 1)

        @block.gpsimd
        def _(pool):
            pool.memset(ident[:], 0.0).then_inc(s["pool_chain"], 1)
            pool.wait_ge(s["pool_chain"], 1)
            pool.affine_select(out=ident[:], in_=ident[:], compare_op=ALU.not_equal, fill=1.0, base=0,
                               pattern=[[-1, P]], channel_multiplier=1).then_inc(s["pool_setup"], 1)
            pool.memset(half[:], -0.5).then_inc(s["pool_chain"], 1)
            n = 2
            if lengths:
                pool.memset(head_of[:], 1.0).then_inc(s["head_chain"], 1)
                pool.wait_ge(s["head_chain"], 1)
                pool.affine_select(out=head_of[:], in_=head_of[:], compare_op=ALU.is_ge, fill=0.0, base=0,
                                   pattern=[[-DH, HC]], channel_multiplier=1).then_inc(s["head_chain"], 1)
                pool.wait_ge(s["head_chain"], 2)
                pool.affine_select(out=head_of[:], in_=head_of[:], compare_op=ALU.is_ge, fill=0.0, base=DH - 1,
                                   pattern=[[DH, HC]], channel_multiplier=-1).then_inc(s["pool_setup"], 1)
            if causal:
                pool.iota(iota_i[:, 0:P], pattern=[[1, P]], base=0, channel_multiplier=0).then_inc(s["pool_chain"], 1)
                pool.iota(iota_i[:, P:3 * P], pattern=[[1, S]], base=0, channel_multiplier=0
                          ).then_inc(s["pool_chain"], 1)
                pool.wait_ge(s["pool_chain"], 4)
                pool.tensor_copy(key[:], iota_i[:]).then_inc(s["pool_chain"], 1)
                pool.wait_ge(s["pool_chain"], 5)
                pool.affine_select(out=key[:, 0:P], in_=key[:, 0:P], compare_op=ALU.is_ge, fill=BEYOND, base=0,
                                   pattern=[[-1, P]], channel_multiplier=1).then_inc(s["pool_setup"], 1)
                pool.affine_select(out=key[:, P:3 * P], in_=key[:, P:3 * P], compare_op=ALU.is_ge, fill=BEYOND,
                                   base=P, pattern=[[-1, S]], channel_multiplier=1).then_inc(s["pool_setup"], 1)
                n = 5
            elif cross:
                pool.iota(iota_i[:], pattern=[[1, S]], base=0, channel_multiplier=0).then_inc(s["pool_chain"], 1)
                pool.wait_ge(s["pool_chain"], 3)
                pool.tensor_copy(key[:], iota_i[:]).then_inc(s["pool_setup"], 1)
                n = 3
            pool.wait_ge(s["pool_chain"], n)

            def norm_factors(b):
                pool.wait_ge(s["var_ready"], b + 1)
                pool.tensor_tensor(rstd[:], rstd[:], half[:], ALU.pow).then_inc(s["rstd_ready"], 1)
                hold(pool, s["rstd_ready"], b + 1, s)

            def normalise(b, tiles):
                for i in tiles:
                    t = (x_in if i < 2 else c_in)[:, i % 2]
                    if i == 2:
                        pool.sem_inc(s["held"], 1)
                    pool.tensor_scalar(t, t, mv[:, i, 0:1], rstd[:, i:i + 1], ALU.subtract, ALU.mult
                                       ).then_inc(s["x_ready"], 1)
                pool.wait_ge(s["x_ready"], 4 * b + tiles[-1] + 1)

            def front(b):
                if masked_ctx:
                    norm_factors(b)
                    normalise(b, (0, 1))
                    normalise(b, (2, 3))
                if cross:
                    pool.wait_ge(s["c_loaded"], IT * (b + 1))
                    hold(pool, s["x_seen"], b + 1, s)
                    for t in range(TT):
                        pool.tensor_scalar(c_in[:, t], c_in[:, t], m_next[:, t:t + 1], None, ALU.mult
                                           ).then_inc(s["c_masked"], 1)
                    pool.wait_ge(s["c_masked"], TT * (b + 1))

            def keys_lo(b, c):
                pool.wait_ge(s["k_hi"], KC * b + c + 1)
                r = c % 2
                for j in (2, 3):
                    part = slice(j * DH, (j + 1) * DH)
                    pool.tensor_tensor(K[1][part, r, j, :], K32[part, :], K[0][part, r, j, :].bitcast(F32),
                                             ALU.subtract).then_inc(s["k_lo_pool"], 1)
                    pool.wait_ge(s["k_lo_pool"], 2 * (KC * b + c) + j - 1)

            def power(b, i):
                n = 2 if cross else 1
                pool.wait_ge(s["lnvar"], n * (b - 1) + i + 1)
                pool.tensor_tensor(rstd[:], rstd[:], half[:], ALU.pow).then_inc(s["lnrstd"], 1)
                pool.wait_ge(s["lnrstd"], n * (b - 1) + i + 1)
                if i == n - 1:
                    pool.tensor_tensor(offset[:], minus_mean[:], rstd[:], ALU.mult).then_inc(s["offset_ready"], 1)

            def last_norm(b):
                gain, shift = (g3, b3) if cross else (g_rep, b_rep)
                pool.wait_ge(s["normalised"], b)
                for t in range(TT):
                    pool.tensor_tensor(res[:, t], res[:, t], gain[:], ALU.mult).then_inc(s["gained"], 1)
                for t in range(TT):
                    pool.wait_ge(s["gained"], TT * (b - 1) + t + 1)
                    ins = pool.tensor_tensor(res[:, t], res[:, t], shift[:], ALU.add)
                ins.then_inc(s["out_ready"], 1)
                pool.wait_ge(s["out_ready"], b)

            def turn(b, prev=True, cur=True, nxt=True):
                if masked_ctx:
                    if prev:
                        pool.wait_ge(s["res_loaded"], IT * b)
                        for t in range(TT):
                            pool.tensor_tensor(res[:, t], res[:, t], p_bias[:], ALU.add).then_inc(s["res_biased"], 1)
                        pool.wait_ge(s["res_biased"], TT * b)
                    if cur:
                        keys_lo(b, 1)
                    if nxt:
                        norm_factors(b + 1)
                        normalise(b + 1, (0, 1))
                    if cur:
                        keys_lo(b, 2)
                    if nxt:
                        normalise(b + 1, (2, 3))
                    if cur:
                        keys_lo(b, 3)
                    if nxt:
                        keys_lo(b + 1, 0)
                    return
                if cur:
                    keys_lo(b, 1)
                if cross and prev:
                    power(b, 0)
                if cur:
                    keys_lo(b, 2)
                if cross and nxt:
                    front(b + 1)
                if causal and prev:
                    power(b, 0)
                    last_norm(b)
                if cur:
                    keys_lo(b, 3)
                if nxt:
                    keys_lo(b + 1, 0)
                if cross and prev:
                    power(b, 1)
                    last_norm(b)

            front(0)
            pool.wait_ge(s["vec_loaded"], IT * NV)
            keys_lo(0, 0)
            turn(0, prev=False)
            with pool.Fori(1, B - 1) as b:
                turn(b)
            turn(B - 1, nxt=False)
            turn(B, cur=False, nxt=False)

        @block.scalar
        def _(act):
            if masked_ctx:
                act.wait_ge(s["vec_loaded"], IT * NV)
                act.wait_ge(s["setup"], 1)

            def matrix_hi(i):
                act.wait_ge(s[f"stage_loaded{i % 2}"], IT * (i // 2 + 1))
                st = stage[:, i % 2]
                for k in range(KC):
                    if masked_ctx and i < 3:
                        sc = wq_scale[:, k:k + 1] if i == 0 else wcol[:, 2, k:k + 1]
                        ins = act.activation(W[0][:, i, k], st[:, k], ACT.Identity, scale=sc)
                    else:
                        ins = act.activation(W[0][:, i, k], st[:, k], ACT.Copy, scale=-SCALE if i == 0 else 1.0)
                ins.then_inc(s["w_hi_done"], 1)

            def turned(b, k):
                act.wait_ge(s["t_ps"], NP * b + k + 1)
                to = (xT if k < 2 else cT)[0][:, 2 * (k % 2):2 * (k % 2) + 2, :]
                act.activation(to, X[T_BANK[k]][:].rearrange("p (c t) -> p c t", c=2), ACT.Copy
                               ).then_inc(s["t_hi"], 1)

            def qk(b, c):
                act.wait_ge(s["qk_ps"], KC * b + c + 1)
                if masked_ctx:
                    act.activation(K32[:], G[:, S:2 * S], ACT.Identity, bias=qk_bias[:, 1, c:c + 1])
                    ins = act.activation(Q[0][:, c % 2, :], G[:, 0:S], ACT.Identity, bias=qk_bias[:, 0, c:c + 1])
                else:
                    act.activation(K32[:], G[:, S:2 * S], ACT.Copy)
                    ins = act.activation(Q[0][:, c % 2, :], G[:, 0:S], ACT.Copy)
                ins.then_inc(s["qk_hi"], 1)

            def values(b, h):
                if not masked_ctx:
                    act.wait_ge(s["v_ps"], 2 * b + h + 1)
                    if not isinstance(b, int) or b > 0:
                        act.wait_ge(s["av_done"], PAIRS * b - PAIRS // 2 * (1 - h))
                    for t in range(TT):
                        ins = act.activation(V[:, t, h * H // 2:(h + 1) * H // 2, 0:DH],
                                             X[VB_BANK if h else VA_BANK][:, t * HALF:(t + 1) * HALF]
                                             .rearrange("p (h d) -> p h d", d=DH), ACT.Copy)
                    ins.then_inc(s["v_ready"], 1)

            def width(u):
                return P if causal and (u // 2) % 2 == 0 else S

            def exps(b, u):
                act.wait_ge(s["masked"], UNITS * b + u + 1)
                if u >= 2 or not isinstance(b, int) or b > 0:
                    act.wait_ge(s["pt_ready"], UNITS * b + u - 1)
                w = width(u)
                c, qt, pr = u // 4, (u // 2) % 2, u % 2
                for j in range(2):
                    ins = act.activation(prob[:, u % 2, j, 0:w], SC[u % 2][:, j * w:(j + 1) * w], ACT.Exp,
                                         bias=low[:, u % 4, j:j + 1], scale=-1.0,
                                         accum_out=sums[:, c, qt, 2 * pr + j:2 * pr + j + 1])
                ins.then_inc(s["exp_done"], 1)

            def attended(b, c):
                act.wait_ge(s["av_done"], PAIRS * b + 2 * (c + 1))
                act.activation(OT[:], O[:, 0:S], ACT.Copy).then_inc(s["ot_done"], 1)

            def copy(b, u):
                act.wait_ge(s["pt_ready"], UNITS * b + u + 1)
                n = 2 * width(u)
                act.activation(probT[:, u % 4, 0:n], PT[u % NPT][:, 0:n], ACT.Copy).then_inc(s["copied"], 1)

            def post_hi(b, p, bank):
                act.wait_ge(s["post_ps"], 2 * (b - 1) + p + 1)
                act.activation((zT if masked_ctx else x2T)[0][:, 2 * p:2 * p + 2, :],
                               X[bank][:].rearrange("p (c t) -> p c t", c=2), ACT.Copy).then_inc(s["post_hi"], 1)

            def normalise(b):
                act.wait_ge(s["offset_ready"], b)
                for t in range(TT):
                    ins = act.activation(res[:, t], res[:, t], ACT.Identity, scale=rstd[:, t:t + 1],
                                         bias=offset[:, t:t + 1])
                ins.then_inc(s["normalised"], 1)

            def relu(b, p):
                act.wait_ge(s["f1_ps"], 2 * (b - 1) + p + 1)
                for i in range(2):
                    m = 2 * p + i
                    ins = act.activation(h32[:, m, :], X[1][:, i * S:(i + 1) * S], ACT.Relu, bias=f1b[:, m:m + 1])
                ins.then_inc(s["f1_act"], 1)

            def turn(b, prev=True, cur=True, nxt=True):
                for t in range(UNITS):
                    if prev and t < 2 or cur and t >= 2:
                        copy(b, t - 2)
                    if cross and prev and t in (9, 10):
                        relu(b, t - 9)
                    if cur:
                        exps(b, t)
                    if t % 4 == 3 and (prev if t < 4 else cur):
                        attended(b, (t - 7) // 4)
                    if cur and t in (0, 4, 8):
                        qk(b, t // 4 + 1)
                    if nxt and t == 12:
                        qk(b + 1, 0)
                    if cur and t == (6 if causal else 5):
                        values(b, 1)
                    if nxt and t == (15 if cross else 14):
                        values(b + 1, 0)
                    if masked_ctx:
                        if prev and t in (5, 6):
                            post_hi(b, t - 5, 1 if t == 5 else 0)
                        if nxt and t in (8, 9, 10):
                            for k in {8: (0, 1), 9: (2,), 10: (3,)}[t]:
                                turned(b + 1, k)
                    if causal and nxt and t == 9:
                        turned(b + 1, 0)
                        turned(b + 1, 1)
                    if lengths and prev and t == (15 if cross else 8):
                        normalise(b)
                    if cross:
                        if prev and t == 7:
                            post_hi(b, 0, 1)
                            post_hi(b, 1, 0)
                        if nxt and t in (8, 9):
                            turned(b + 1, t - 8)
                        if nxt and t == 10:
                            turned(b + 1, 2)
                            turned(b + 1, 3)

            for i in range(min(NM, 3)):
                matrix_hi(i)
            for k in range(NP):
                turned(0, k)
            for i in range(3, NM):
                matrix_hi(i)
            act.wait_ge(s["vec_loaded"], IT * NV)
            act.wait_ge(s["setup"], 2)
            if masked_ctx:
                act.wait_ge(s["bias_done"], 3)
            qk(0, 0)
            values(0, 0)
            turn(0, prev=False)
            with act.Fori(1, B - 1) as b:
                turn(b)
            turn(B - 1, nxt=False)
            turn(B, cur=False, nxt=False)

        @block.vector
        def _(dve):
            head = {"mask": 6, "causal": 20, "cross": 19}[kind]
            per = {"mask": 6, "causal": 26, "cross": 32}[kind]
            chain = Chain(dve, s["chain"], head, per)
            if masked_ctx:
                dve.wait_ge(s["vec_loaded"], IT * NV)
                dve.tensor_scalar(wq_scale[:], wcol[:, 0, :], -SCALE, None, ALU.mult).then_inc(s["setup"], 1)
            else:
                dve.sem_inc(s["setup"], 1)
            for part in range(2):
                dve.memset(K[part][:].bitcast(F32), 0.0)
            if masked_ctx:
                dve.memset(bias_rep[:], 1.0).then_inc(s["setup"], 1)
            else:
                dve.memset(ones[:], 1.0)
                dve.memset(big[:], BIG).then_inc(s["setup"], 1)
            dve.wait_ge(s["setup"], 2)
            if masked_ctx:
                for k in range(KC):
                    ins = dve.tensor_scalar(bias_rep[:, k, :], bias_rep[:, k, :], wcol[:, 3, k:k + 1], None, ALU.mult)
                ins.then_inc(s["setup"], 1)

            def matrix_lo(i):
                dve.wait_ge(s["w_hi_done"], i + 1)
                st = stage[:, i % 2]
                hi = W[0][:, i].bitcast(F32)
                for k in range(KC):
                    if masked_ctx and i < 3:
                        sc = wq_scale[:, k:k + 1] if i == 0 else wcol[:, 2, k:k + 1]
                    else:
                        sc = -SCALE if i == 0 else 1.0
                    ins = dve.scalar_tensor_tensor(out=W[1][:, i, k], in0=st[:, k], scalar=sc, in1=hi[:, k],
                                                   op0=ALU.mult, op1=ALU.subtract)
                ins.then_inc(s["w_lo_done"], 1)
                if masked_ctx and i < 3:
                    dve.wait_ge(s["bias_ps"], i + 1)
                    if i == 0:
                        dve.tensor_scalar(qk_bias[:, 0, :], G[:, 0:KC], -SCALE, None, ALU.mult
                                          ).then_inc(s["bias_done"], 1)
                    elif i == 1:
                        dve.tensor_copy(qk_bias[:, 1, :], G[:, 0:KC]).then_inc(s["bias_done"], 1)
                    else:
                        dve.tensor_copy(v_bias[:], O[:]).then_inc(s["bias_done"], 1)

            def front(b):
                if masked_ctx:
                    dve.wait_ge(s["x_loaded"], IT * (b + 1))
                    dve.wait_ge(s["c_loaded"], IT * (b + 1))
                    for i in range(4):
                        ins = dve.bn_stats(stats[:, i, :], (x_in if i < 2 else c_in)[:, i % 2])
                    chain.done(ins)
                    chain.hold(s)
                    for i in range(4):
                        ins = dve.bn_aggr(mv[:, i, :], stats[:, i, :])
                    chain.done(ins)
                    chain.wait()
                    dve.tensor_scalar(rstd[:], mv[:, :, 1], EPS, None, ALU.add).then_inc(s["var_ready"], 1)
                else:
                    dve.wait_ge(s["x_loaded"], IT * (b + 1))
                    chain.done(dve.tensor_reduce(big[:], x_in[:], AX_X, ALU.max, apply_absolute_value=True))
                    chain.wait()
                    dve.tensor_scalar(m_next[:], big[:], 0.0, None, ALU.not_equal).then_inc(s["x_seen"], 1)

            def turned(b, k):
                dve.wait_ge(s["t_hi"], NP * b + k + 1)
                dst_t = (xT if k < 2 else cT)
                sl = slice(2 * (k % 2), 2 * (k % 2) + 2)
                dve.tensor_tensor(dst_t[1][:, sl, :], X[T_BANK[k]][:].rearrange("p (c t) -> p c t", c=2),
                                  dst_t[0][:, sl, :].bitcast(F32), ALU.subtract).then_inc(s["t_lo"], 1)

            def query0(b, c):
                dve.wait_ge(s["qk_hi"], KC * b + c + 1)
                dve.tensor_scalar(Q0[:], head_of[:], G[:, 0:1], None, ALU.mult).then_inc(s["e0_in"], 1)

            def keys_hi(b, c):
                r = c % 2
                dve.wait_ge(s["qk_hi"], KC * b + c + 1)
                for j in range(HC):
                    part = slice(j * DH, (j + 1) * DH)
                    ins = dve.tensor_copy(K[0][part, r, j, :], K32[part, :])
                ins.then_inc(s["k_hi"], 1)

            def queries_lo(b, c):
                r = c % 2
                if masked_ctx:
                    dve.scalar_tensor_tensor(out=Q[1][:, r, :], in0=G[:, 0:S], scalar=qk_bias[:, 0, c:c + 1],
                                             in1=Q[0][:, r, :].bitcast(F32), op0=ALU.add, op1=ALU.subtract
                                             ).then_inc(s["q_lo"], 1)
                else:
                    dve.tensor_tensor(Q[1][:, r, :], G[:, 0:S], Q[0][:, r, :].bitcast(F32), ALU.subtract
                                      ).then_inc(s["q_lo"], 1)

            def keys_lo(b, c):
                r = c % 2
                dve.wait_ge(s["k_hi"], KC * b + c + 1)
                for j in (0, 1):
                    part = slice(j * DH, (j + 1) * DH)
                    ins = dve.tensor_tensor(K[1][part, r, j, :], K32[part, :], K[0][part, r, j, :].bitcast(F32),
                                            ALU.subtract)
                ins.then_inc(s["k_lo"], 1)

            def nonzero(b, c):
                dve.wait_ge(s["e0_ps"], KC * b + c + 1)
                dve.tensor_scalar(flags[:].rearrange("p t h -> p (t h)"), M[:, 0:TT * HC], 0.0, None, ALU.not_equal
                                  ).then_inc(s["flags_done"], 1)

            def cuts(b, c):
                r = c % 2
                dve.wait_ge(s["len_ps"], KC * b + c + 1)
                dve.tensor_copy(lens[:], M[:, 16:16 + HC]).then_inc(s["len_read"], 1)
                dve.wait_ge(s["len_read"], KC * b + c + 1)
                chain.done(dve.reciprocal(rlen[:], lens[:]))
                chain.wait()
                dve.tensor_scalar(nan0[:, c, :], rlen[:], 0.0, None, ALU.mult)
                for j in range(HC):
                    ins = dve.tensor_scalar(cut[:, r, j, :], key[:], lens[:, j:j + 1], BIG, ALU.is_ge, ALU.mult)
                chain.done(ins)
                chain.hold(s)

            def values(b, h):
                dve.wait_ge(s["v_ps"], 2 * b + h + 1)
                if not isinstance(b, int) or b > 0:
                    dve.wait_ge(s["av_done"], PAIRS * b - PAIRS // 2 * (1 - h))
                for t in range(TT):
                    ins = dve.tensor_tensor(V[:, t, h * H // 2:(h + 1) * H // 2, 0:DH],
                                            X[VB_BANK if h else VA_BANK][:, t * HALF:(t + 1) * HALF]
                                            .rearrange("p (h d) -> p h d", d=DH),
                                            v_bias[:, h * HALF:(h + 1) * HALF].rearrange("p (h d) -> p h d", d=DH),
                                            ALU.add)
                ins.then_inc(s["v_ready"], 1)

            def mask_floats(b):
                dve.wait_ge(s["m_loaded"], IT * (b + 1))
                if not isinstance(b, int) or b > 0:
                    dve.wait_ge(s["masked"], UNITS * b)
                dve.tensor_scalar(mask[:], m_in[:], F32_MAX, None, ALU.mult).then_inc(s["m_ready"], 1)

            def masks_and_minima(b, u):
                c, qt, pr = u // 4, (u // 2) % 2, u % 2
                if masked_ctx and u == 0:
                    dve.wait_ge(s["m_ready"], b + 1)
                hold(dve, s["s_ready"], UNITS * b + u + 1, s)
                for j in range(2):
                    if masked_ctx:
                        w, extra = S, mask[:, qt, :]
                    elif causal:
                        w = P if qt == 0 else S
                        extra = cut[:, c % 2, 2 * pr + j, (P if qt else 0):(3 * P if qt else P)]
                    else:
                        w, extra = S, cut[:, c % 2, 2 * pr + j, :]
                    sc = SC[u % 2][:, j * w:(j + 1) * w]
                    ins = dve.tensor_tensor_reduce(sc, sc, extra, 1.0, F32_MAX, ALU.add, ALU.min,
                                                   low[:, u % 4, j:j + 1])
                ins.then_inc(s["masked"], 1)

            def attended(b, c):
                dve.wait_ge(s["z_ps"], KC * b + c + 1)
                chain.done(dve.reciprocal(rs[:], sums[:, c]))
                chain.wait()
                if lengths:
                    for t in range(TT):
                        ins = dve.tensor_tensor(rs[:, t, :], rs[:, t, :], nan0[:, c, :], ALU.add)
                    chain.done(ins)
                    chain.wait()
                    for t in range(TT):
                        ins = dve.tensor_scalar(rs[:, t, :], rs[:, t, :], m_cur[:, t:t + 1], None, ALU.mult)
                    chain.done(ins)
                    chain.wait()
                dve.tensor_tensor(z[:, :, c * P:(c + 1) * P].rearrange("p t (h d) -> p t h d", h=HC),
                                  Oz, rs[:].unsqueeze(3).to_broadcast([P, TT, HC, DH]), ALU.mult
                                  ).then_inc(s["z_done"], 1)

            def ln_var(b):
                for t in range(TT):
                    ins = dve.bn_aggr(mv[:, t, :], stats[:, t, :])
                chain.done(ins)
                chain.wait()
                dve.tensor_scalar(minus_mean[:], mv[:, :, 0], -1.0, None, ALU.mult)
                dve.tensor_scalar(rstd[:], mv[:, :, 1], EPS, None, ALU.add).then_inc(s["lnvar"], 1)

            def ln_gain(gain):
                for t in range(TT):
                    ins = dve.scalar_tensor_tensor(out=res[:, t], in0=res[:, t], scalar=mv[:, t, 0:1], in1=gain[:],
                                                   op0=ALU.subtract, op1=ALU.mult)
                chain.done(ins)
                chain.wait()

            def ln_shift(b, i, shift):
                dve.wait_ge(s["lnrstd"], (2 if cross else 1) * (b - 1) + i + 1)
                for t in range(TT):
                    ins = dve.scalar_tensor_tensor(out=res[:, t], in0=res[:, t], scalar=rstd[:, t:t + 1],
                                                   in1=shift[:], op0=ALU.mult, op1=ALU.add)
                return ins

            def add_z(b):
                dve.wait_ge(s["res_loaded"], IT * b)
                dve.wait_ge(s["z_done"], KC * b + 1)
                for t in range(TT):
                    ins = dve.tensor_tensor(res[:, t], res[:, t], z[:, t], ALU.add)
                chain.done(ins)
                chain.wait()
                for t in range(TT):
                    ins = dve.bn_stats(stats[:, t, :], res[:, t])
                chain.done(ins)
                chain.hold(s)

            def norm_z(b, stage):
                if stage == 0:
                    add_z(b)
                elif stage == 1:
                    ln_var(b)
                    if cross:
                        ln_gain(g_rep)
                elif cross:
                    ln_shift(b, 0, b_rep).then_inc(s["res_done"], 1)

            def post_lo(b, p, bank):
                to = zT if masked_ctx else x2T
                dve.wait_ge(s["post_hi"], 2 * (b - 1) + p + 1)
                dve.tensor_tensor(to[1][:, 2 * p:2 * p + 2, :], X[bank][:].rearrange("p (c t) -> p c t", c=2),
                                  to[0][:, 2 * p:2 * p + 2, :].bitcast(F32), ALU.subtract).then_inc(s["post_lo"], 1)

            def project(b, t):
                dve.wait_ge(s["proj_ps"], TT * (b - 1) + t + 1)
                if t == 0:
                    dve.wait_ge(s["res_biased"], TT * b)
                dve.tensor_tensor(res[:, t], X[1 - t][:], res[:, t], ALU.add).then_inc(s["proj_read"], 1)
                if t == 1:
                    dve.wait_ge(s["proj_read"], TT * b + 1)
                    dve.sem_inc(s["out_ready"], 1)

            def hidden_parts(b, p):
                sl = slice(2 * p, 2 * p + 2)
                dve.wait_ge(s["f1_act"], 2 * (b - 1) + p + 1)
                dve.tensor_copy(hT[0][:, sl, :], h32[:, sl, :]).then_inc(s["f1_hi"], 1)
                dve.wait_ge(s["f1_hi"], 2 * (b - 1) + p + 1)
                dve.tensor_tensor(hT[1][:, sl, :], h32[:, sl, :], hT[0][:, sl, :].bitcast(F32), ALU.subtract
                                  ).then_inc(s["f1_lo"], 1)

            def fed(b, t):
                y = h32[:].rearrange("p (t k) s -> p t (k s)", t=TT)
                dve.wait_ge(s["proj_ps"], TT * (b - 1) + t + 1)
                dve.wait_ge(s["f1_lo"], 2 * b)
                dve.tensor_tensor(y[:, t], X[t][:], f2b[:], ALU.add).then_inc(s["proj_read"], 1)
                dve.wait_ge(s["proj_read"], TT * (b - 1) + t + 2)
                chain.done(dve.scalar_tensor_tensor(out=res[:, t], in0=y[:, t], scalar=m0[:, t:t + 1],
                                                    in1=res[:, t], op0=ALU.mult, op1=ALU.add))
                chain.wait()
                chain.done(dve.bn_stats(stats[:, t, :], res[:, t]))
                if t == TT - 1:
                    chain.hold(s)

            def rows_kept(b):
                chain.done(dve.tensor_copy(m_cur[:], m_next[:]))
                if causal:
                    chain.done(dve.tensor_copy(keep[:, bass.ds(b * TT, TT)], m_next[:]))
                chain.wait()

            def turn(b, prev=True, cur=True, nxt=True):
                if prev and cur:
                    chain.turn(b)
                for t in range(UNITS):
                    c, i = t // 4, t % 4
                    ahead = (b, c + 1) if c + 1 < KC else (b + 1, 0)
                    is_ahead = cur if c + 1 < KC else nxt
                    if t == 0 and masked_ctx and cur:
                        mask_floats(b)
                    if lengths and i == 3 and is_ahead:
                        nonzero(*ahead)
                    if i == 3 and is_ahead:
                        keys_lo(*ahead)
                    if prev and masked_ctx:
                        if t in (6, 7):
                            post_lo(b, t - 6, 1 if t == 6 else 0)
                        if t == 8:
                            project(b, 0)
                        if t == 13:
                            project(b, 1)
                    if nxt:
                        for k in {"mask": {9: (0, 1), 10: (2,), 11: (3,)}, "causal": {10: (0, 1)},
                                  "cross": {9: (0,), 10: (1,), 11: (2, 3)}}[kind].get(t, ()):
                            turned(b + 1, k)
                    if prev and cross:
                        if t == 15:
                            ln_var(b)
                        if t == 8:
                            post_lo(b, 0, 1)
                            post_lo(b, 1, 0)
                    if cur:
                        masks_and_minima(b, t)
                    if i == 0 and (prev if c < 2 else cur):
                        attended(b - 1 if c < 2 else b, (c - 2) % KC)
                    if lengths and i == 1 and is_ahead:
                        query0(*ahead)
                    if i == 1 and is_ahead:
                        keys_hi(*ahead)
                    if i == 2 and is_ahead:
                        queries_lo(*ahead)
                    if lengths and i == 3 and is_ahead:
                        cuts(*ahead)
                    if prev and cross and t in (4, 5, 6):
                        norm_z(b, t - 4)
                    if prev and causal and t in (5, 7):
                        norm_z(b, (t - 5) // 2)
                    if lengths and cur and t == 4:
                        rows_kept(b)
                    if nxt and t == {"mask": 3, "causal": 14, "cross": 8}[kind]:
                        front(b + 1)
                    if masked_ctx and cur and t == 5:
                        values(b, 1)
                    if masked_ctx and nxt and t == 14:
                        values(b + 1, 0)
                    if prev and cross:
                        if t == 7:
                            chain.done(dve.tensor_copy(m0[:], keep[:, bass.ds((b - 1) * TT, TT)]))
                            chain.wait()
                        if t in (10, 11):
                            hidden_parts(b, t - 10)
                        if t in (13, 14):
                            fed(b, t - 13)

            dve.sem_inc(s["z_done"], 1)
            dve.sem_inc(s["proj_read"], 1)
            front(0)
            for i in range(min(NM, 3)):
                matrix_lo(i)
            for k in range(NP):
                turned(0, k)
            for i in range(3, NM):
                matrix_lo(i)
            dve.wait_ge(s["vec_loaded"], IT * NV)
            if lengths:
                dve.wait_ge(s["pool_setup"], 4 if causal else 3)
                query0(0, 0)
            keys_hi(0, 0)
            queries_lo(0, 0)
            keys_lo(0, 0)
            if masked_ctx:
                values(0, 0)
            if lengths:
                nonzero(0, 0)
                cuts(0, 0)
            turn(0, prev=False)
            with dve.Fori(1, B - 1) as b:
                turn(b)
            turn(B - 1, nxt=False)
            turn(B, cur=False, nxt=False)

        @block.tensor
        def _(pe):
            pe.wait_ge(s["pool_setup"], 1)
            if masked_ctx:
                pe.wait_ge(s["vec_loaded"], IT * NV)
                pe.wait_ge(s["setup"], 3)
                for i in range(3):
                    pe.wait_ge(s[f"stage_loaded{i % 2}"], IT * (i // 2 + 1))
                    if i < 2:
                        if i:
                            pe.wait_ge(s["bias_done"], i)
                        for m in range(KC):
                            for k in range(KC):
                                ins = pe.matmul(G[:, m:m + 1], stage[:, i % 2, k, m * P:(m + 1) * P],
                                                wcol[:, 1 if i == 0 else 3, k:k + 1],
                                                start=(k == 0), stop=(k == KC - 1))
                    else:
                        for k in range(KC):
                            ins = pe.matmul(O[:], bias_rep[:, k, :], stage[:, i % 2, k, :],
                                            start=(k == 0), stop=(k == KC - 1))
                    ins.then_inc(s["bias_ps"], 1)

            def turn_over(b, k):
                src = x_in if k < 2 else c_in
                if k % 2 == 0:
                    if masked_ctx:
                        pe.wait_ge(s["x_ready"], 4 * b + k + 2)
                    elif k == 0:
                        pe.wait_ge(s["x_loaded"], IT * (b + 1))
                    else:
                        pe.wait_ge(s["c_masked"], TT * (b + 1))
                back = {"mask": (0, 0, 1, 2), "causal": (0, 0), "cross": (0, 1, 2, 0)}[kind][k]
                if back:
                    pe.wait_ge(s["t_lo"], NP * b + back)
                for i in range(2):
                    ch = 2 * (k % 2) + i
                    for t in range(TT):
                        ins = pe.transpose(X[T_BANK[k]][:, i * S + t * P:i * S + (t + 1) * P],
                                           src[:, t, ch * P:(ch + 1) * P], ident[:])
                ins.then_inc(s["t_ps"], 1)

            def values(b, h):
                for t in range(TT):
                    ins = product(pe, X[VB_BANK if h else VA_BANK][:, t * HALF:(t + 1) * HALF],
                                  lambda k, a: cT[a][:, k, t * P:(t + 1) * P],
                                  lambda k, c: W[c][:, 2, k, h * HALF:(h + 1) * HALF])
                ins.then_inc(s["v_ps"], 1)

            def queries(b, c):
                if c == 0:
                    pe.wait_ge(s["t_lo"], NP * b + 2)
                if c > 0 or not isinstance(b, int) or b > 0:
                    pe.wait_ge(s["q_lo"], KC * b + c)
                product(pe, G[:, 0:S], lambda k, a: W[a][:, 0, k, c * P:(c + 1) * P], lambda k, p: xT[p][:, k, :])

            def keys(b, c):
                if c == 0:
                    pe.wait_ge(s["t_lo"], NP * (b + 1))
                product(pe, G[:, S:2 * S], lambda k, a: W[a][:, 1, k, c * P:(c + 1) * P],
                        lambda k, p: cT[p][:, k, :]).then_inc(s["qk_ps"], 1)

            def energies0(b, c):
                pe.wait_ge(s["e0_in"], KC * b + c + 1)
                for kt in range(TT):
                    ins = pe.matmul(M[:, kt * HC:(kt + 1) * HC], K32[:, kt * P:(kt + 1) * P], Q0[:],
                                    start=True, stop=True)
                ins.then_inc(s["e0_ps"], 1)

            def count(b, c):
                pe.wait_ge(s["flags_done"], KC * b + c + 1)
                for kt in range(TT):
                    ins = pe.matmul(M[:, 16:16 + HC], ones[:], flags[:, kt, :], start=(kt == 0), stop=(kt == TT - 1))
                ins.then_inc(s["len_ps"], 1)

            def scores(b, u):
                c, qt, pr = u // 4, (u // 2) % 2, u % 2
                w = P if causal and qt == 0 else S
                if u % 4 == 0:
                    pe.wait_ge(s["q_lo"], KC * b + c + 1)
                    pe.wait_ge(s["k_lo"], KC * b + c + 1)
                    pe.wait_ge(s["k_lo_pool"], 2 * (KC * b + c + 1))
                if u >= 2 or not isinstance(b, int) or b > 0:
                    pe.wait_ge(s["exp_done"], UNITS * b + u - 1)
                n = 0
                for a, k in PASSES:
                    ins = pe.matmul(SC[u % 2][:, 0:2 * w].rearrange("p (h k) -> p h k", h=2),
                                    Q[a][:, c % 2, qt * P:(qt + 1) * P], K[k][:, c % 2, 2 * pr:2 * pr + 2, 0:w],
                                    start=(n == 0), stop=(n == 2))
                    n += 1
                ins.then_inc(s["s_ready"], 1)

            def turn_probs(b, u):
                w = P if causal and (u // 2) % 2 == 0 else S
                pe.wait_ge(s["exp_done"], UNITS * b + u + 1)
                if u >= NPT or not isinstance(b, int) or b > 0:
                    pe.wait_ge(s["copied"], UNITS * b + u + 1 - NPT)
                n = 0
                for j in range(2):
                    for kt in range(w // P):
                        ins = pe.transpose(PT[u % NPT][:, n * P:(n + 1) * P], prob[:, u % 2, j, kt * P:(kt + 1) * P],
                                           ident[:])
                        n += 1
                ins.then_inc(s["pt_ready"], 1)

            def attend(b, m):
                c, qt = m // 2, m % 2
                nk = 1 if causal and qt == 0 else TT
                pe.wait_ge(s["copied"], UNITS * b + 2 * m + 2)
                if m in (0, PAIRS // 2):
                    pe.wait_ge(s["v_ready"], 2 * b + (2 if m else 1))
                if qt == 0:
                    pe.wait_ge(s["z_done"], KC * b + c + 1)
                for kt in range(nk):
                    for hh in range(HC):
                        u, j = 2 * m + hh // 2, hh % 2
                        ins = pe.matmul(O[hh * DH:(hh + 1) * DH, qt * P:(qt + 1) * P],
                                        V[:, kt, HC * (c % KC) + hh, :],
                                        probT[:, u % 4, (j * nk + kt) * P:(j * nk + kt + 1) * P],
                                        start=(kt == 0), stop=(kt == nk - 1))
                ins.then_inc(s["av_done"], 1)

            def attended(b, c):
                pe.wait_ge(s["ot_done"], KC * b + c + 1)
                for qt in range(TT):
                    ins = pe.transpose(O[:, S + qt * P:S + (qt + 1) * P], OT[:, qt * P:(qt + 1) * P], ident[:])
                ins.then_inc(s["z_ps"], 1)

            def post_turn(b, p, bank):
                src = z if masked_ctx else res
                if p == 0 and masked_ctx:
                    pe.wait_ge(s["z_done"], KC * b + 1)
                elif p == 0:
                    pe.wait_ge(s["res_done"], b)
                    pe.wait_ge(s["proj_read"], TT * (b - 1) + 1)
                if p == 1:
                    last_v = 2 * b + 2 if not isinstance(b, int) or b < B else 2 * B
                    pe.wait_ge(s["v_ready"], last_v)
                for i in range(2):
                    for t in range(TT):
                        ch = 2 * p + i
                        ins = pe.transpose(X[bank][:, i * S + t * P:i * S + (t + 1) * P],
                                           src[:, t, ch * P:(ch + 1) * P], ident[:])
                ins.then_inc(s["post_ps"], 1)

            def project(b, t):
                pe.wait_ge(s["post_lo"], 2 * b)
                product(pe, X[1 - t][:], lambda k, a: zT[a][:, k, t * P:(t + 1) * P],
                        lambda k, p: W[p][:, 3, k, :]).then_inc(s["proj_ps"], 1)

            def feed1(b, p):
                pe.wait_ge(s["post_lo"], 2 * b)
                if p == 1:
                    pe.wait_ge(s["f1_act"], 2 * (b - 1) + 1)
                for i in range(2):
                    m = 2 * p + i
                    ins = product(pe, X[1][:, i * S:(i + 1) * S], lambda k, a: W[a][:, 3, k, m * P:(m + 1) * P],
                                  lambda k, q: x2T[q][:, k, :])
                ins.then_inc(s["f1_ps"], 1)

            def feed2(b, t):
                pe.wait_ge(s["f1_lo"], 2 * b)
                product(pe, X[t][:], lambda k, a: hT[a][:, k, t * P:(t + 1) * P],
                        lambda k, p: W[p][:, 4, k, :]).then_inc(s["proj_ps"], 1)

            def turn(b, prev=True, cur=True, nxt=True):
                for t in range(UNITS):
                    c, i = t // 4, t % 4
                    ahead = (b, c + 1) if c + 1 < KC else (b + 1, 0)
                    is_ahead = cur if c + 1 < KC else nxt
                    if cur:
                        scores(b, t)
                    if prev and t < 2 or cur and t >= 2:
                        turn_probs(b, t - 2)
                    if t % 2 == 1 and (prev if t < 5 else cur):
                        attend(b, (t - 5) // 2)
                    if i == 0 and (prev if c < 2 else cur):
                        attended(b, c - 2)
                    if lengths and i == 3 and is_ahead:
                        count(*ahead)
                    if i == 0 and is_ahead:
                        keys(*ahead)
                    if i == 3 and t < 8 and cur:
                        queries(b, c + 2)
                    if i == 3 and t > 8 and nxt:
                        queries(b + 1, c - 2)
                    if lengths and i == 2 and is_ahead:
                        energies0(*ahead)
                    if masked_ctx:
                        if t == 4 and cur:
                            if prev:
                                pe.wait_ge(s["proj_read"], TT * (b - 1) + 1)
                            values(b, 1)
                        if t in (5, 6) and prev:
                            post_turn(b, t - 5, 1 if t == 5 else 0)
                        if t == 7 and prev:
                            project(b, 0)
                        if t == 8 and nxt:
                            pe.wait_ge(s["v_ready"], 2 * b + 2)
                            turn_over(b + 1, 0)
                            if prev:
                                pe.wait_ge(s["proj_read"], TT * (b - 1) + 2)
                            turn_over(b + 1, 1)
                        if t in (9, 10) and nxt:
                            turn_over(b + 1, t - 7)
                        if t == 12 and prev:
                            project(b, 1)
                        if t == 13 and nxt:
                            values(b + 1, 0)
                    if causal:
                        if t == 5 and cur:
                            values(b, 1)
                        if t == 9 and nxt:
                            turn_over(b + 1, 0)
                            pe.wait_ge(s["v_ready"], 2 * b + 2)
                            turn_over(b + 1, 1)
                        if t == 13 and nxt:
                            values(b + 1, 0)
                    if cross:
                        if t == 4 and cur:
                            values(b, 1)
                        if t == 7 and prev:
                            post_turn(b, 0, 1)
                            post_turn(b, 1, 0)
                        if t in (8, 9):
                            if nxt and t == 8:
                                if prev:
                                    pe.wait_ge(s["post_lo"], 2 * b)
                                else:
                                    pe.wait_ge(s["v_ready"], 2 * b + 2)
                            if nxt:
                                turn_over(b + 1, t - 8)
                            if prev:
                                feed1(b, t - 8)
                        if t == 10 and nxt:
                            turn_over(b + 1, 2)
                            if prev:
                                pe.wait_ge(s["f1_act"], 2 * b)
                            turn_over(b + 1, 3)
                        if t in (12, 13) and prev:
                            feed2(b, t - 12)
                        if t == 14 and nxt:
                            if prev:
                                pe.wait_ge(s["proj_read"], TT * (b - 1) + 2)
                            values(b + 1, 0)

            for k in range(NP):
                turn_over(0, k)
            pe.wait_ge(s["w_lo_done"], 1)
            if masked_ctx:
                pe.wait_ge(s["bias_done"], 3)
            queries(0, 0)
            pe.wait_ge(s["w_lo_done"], 2)
            keys(0, 0)
            pe.wait_ge(s["w_lo_done"], 3)
            values(0, 0)
            if lengths:
                pe.wait_ge(s["setup"], 2)
                energies0(0, 0)
                count(0, 0)
            queries(0, 1)
            pe.wait_ge(s["w_lo_done"], NM)
            turn(0, prev=False)
            with pe.Fori(1, B - 1) as b:
                turn(b)
            turn(B - 1, nxt=False)
            turn(B, cur=False, nxt=False)


def mlp_phase(nc, x_src, dst, w1, w2, n_w, n_b, b1, b2):
    NT = 4
    N = NT * P
    TURNS = B * S // N
    MH = HID // P
    x_t = x_src.rearrange("b s c -> (b s) c").rearrange("(n t p) c -> n p t c", t=NT, p=P)
    d_t = dst.rearrange("b s c -> (b s) c").rearrange("(n t p) c -> n p t c", t=NT, p=P)
    with ExitStack() as ctx:
        def sb(name, shape, dt=F32):
            return ctx.enter_context(nc.sbuf_tensor(f"mlp_{name}", shape, dt))

        def bank(name):
            return ctx.enter_context(nc.psum_tensor(f"mlp_{name}", [P, 512], F32))

        W1 = [sb(f"w1_{part}", [P, KC, HID], F32R) for part in ("hi", "lo")]
        W2 = [sb(f"w2_{part}", [P, MH, C], F32R) for part in ("hi", "lo")]
        x = sb("x", [P, NT, C])
        xn = sb("xn", [P, NT, C])
        xT = [sb(f"xT_{part}", [P, KC, N], F32R) for part in ("hi", "lo")]
        h32 = sb("h32", [P, 2, N])
        hT = [sb(f"hT_{part}", [P, 2, N], F32R) for part in ("hi", "lo")]
        y = sb("y", [P, NT, C])
        ident = sb("ident", [P, P])
        ncol = sb("ncol", [P, 2, KC])
        b1col = sb("b1col", [P, MH])
        hb = sb("hb", [P, MH])
        b2r = sb("b2r", [P, C])
        stats = sb("stats", [P, NT, 6])
        mv = sb("mv", [P, NT, 2])
        rstd = sb("rstd", [P, NT])
        half = sb("half", [P, NT])
        ACC = [bank(f"acc{i}") for i in range(NT)]
        F1 = [bank(f"f1_{i}") for i in range(2)]
        TB = [bank(f"turned{i}") for i in range(2)]
        s = Signals(nc, "mlp")
        ctx.callback(s.close)
        pieces = [(w1.rearrange("(k p) n -> p k n", p=P)[:, :, 512 * i:512 * (i + 1)]) for i in range(4)]
        pieces += [(w2.rearrange("(k p) n -> p k n", p=P)[:, 4 * i:4 * i + 4, :]) for i in range(4)]
        stages = [xn, y]

        def part_of(w, i):
            return W1[w][:, :, 512 * i:512 * (i + 1)] if i < 4 else W2[w][:, 4 * (i - 4):4 * (i - 4) + 4, :]

        block = ctx.enter_context(nc.Block())

        @block.sync
        def _(sp):
            for to, frm in ((ncol[:, 0, :], n_w), (ncol[:, 1, :], n_b), (b1col[:], b1),
                            (b2r[:], b2.partition_broadcast(P))):
                sp.dma_start(to, frm).then_inc(s["vec_loaded"], IT)
            sp.dma_start(x[:], x_t[0]).then_inc(s["x_loaded"], IT)
            for i, piece in enumerate(pieces):
                if i >= 2:
                    sp.wait_ge(s["w_lo"], i - 1)
                    if i - 2 < 4:
                        sp.wait_ge(s["bias_ps"], i - 1)
                sp.dma_start(stages[i % 2][:], piece).then_inc(s[f"stage_loaded{i % 2}"], IT)

            def turn(b, last=False):
                if not last:
                    hold(sp, s["xn_ready"], NT * (b + 1), s)
                    hold(sp, s["x_biased"], NT * (b + 1), s)
                    sp.dma_start(x[:], x_t[bass.ds(b + 1, 1)].rearrange("o p t c -> p (o t) c")
                                 ).then_inc(s["x_loaded"], IT)
                hold(sp, s["out_ready"], b + 1, s)
                sp.dma_start(d_t[bass.ds(b, 1)].rearrange("o p t c -> p (o t) c"), y[:]).then_inc(s["stored"], IT)
                hold(sp, s["stored"], IT * (b + 1), s)

            with sp.Fori(0, TURNS - 1) as b:
                turn(b)
            turn(TURNS - 1, last=True)

        @block.gpsimd
        def _(pool):
            pool.memset(ident[:], 0.0).then_inc(s["pool_chain"], 1)
            pool.memset(half[:], -0.5).then_inc(s["pool_chain"], 1)
            pool.wait_ge(s["pool_chain"], 2)
            pool.affine_select(out=ident[:], in_=ident[:], compare_op=ALU.not_equal, fill=1.0, base=0,
                               pattern=[[-1, P]], channel_multiplier=1).then_inc(s["pool_setup"], 1)

            def power(b):
                pool.wait_ge(s["var_ready"], b + 1)
                pool.tensor_tensor(rstd[:], rstd[:], half[:], ALU.pow).then_inc(s["rstd_ready"], 1)

            def residual(b, first=False):
                if not first:
                    pool.wait_ge(s["stored"], IT * b)
                for t in range(NT):
                    pool.tensor_tensor(y[:, t], x[:, t], b2r[:], ALU.add).then_inc(s["x_biased"], 1)

            pool.wait_ge(s["vec_loaded"], 4 * IT)
            power(0)
            pool.wait_ge(s["w_lo"], 8)
            residual(0, first=True)
            with pool.Fori(0, TURNS - 1) as b:
                power(b + 1)
                residual(b + 1)

        @block.scalar
        def _(act):
            act.wait_ge(s["vec_loaded"], 4 * IT)
            for i in range(8):
                act.wait_ge(s[f"stage_loaded{i % 2}"], IT * (i // 2 + 1))
                for k in range(4):
                    src = stages[i % 2][:, k, :]
                    dst_w = part_of(0, i)[:, k, :]
                    if i < 4:
                        ins = act.activation(dst_w, src, ACT.Identity, scale=ncol[:, 0, k:k + 1])
                    else:
                        ins = act.activation(dst_w, src, ACT.Copy)
                ins.then_inc(s["w_hi"], 1)

            def turned(b, k):
                act.wait_ge(s["t_ps"], KC * b + k + 1)
                act.activation(xT[0][:, k, :], TB[k % 2][:], ACT.Copy).then_inc(s["t_hi"], 1)

            def gelu(b, m):
                act.wait_ge(s["f1_ps"], MH * b + m + 1)
                act.activation(h32[:, m % 2, :], F1[m % 2][:], ACT.Gelu, bias=hb[:, m:m + 1]).then_inc(s["gelu"], 1)

            for k in range(KC):
                turned(0, k)
            act.wait_ge(s["bias_done"], 1)
            with act.Fori(0, TURNS - 1) as b:
                for m in range(MH):
                    gelu(b, m)
                for k in range(KC):
                    turned(b + 1, k)
            for m in range(MH):
                gelu(TURNS - 1, m)

        @block.vector
        def _(dve):
            dve.sem_inc(s["acc_read"], 1)

            def norm(b):
                dve.wait_ge(s["x_loaded"], IT * (b + 1))
                for t in range(NT):
                    ins = dve.bn_stats(stats[:, t, :], x[:, t])
                ins.then_inc(s["stats_done"], 1)
                hold(dve, s["stats_done"], b + 1, s)
                for t in range(NT):
                    ins = dve.bn_aggr(mv[:, t, :], stats[:, t, :])
                ins.then_inc(s["mv_done"], 1)
                dve.wait_ge(s["mv_done"], b + 1)
                dve.tensor_scalar(rstd[:], mv[:, :, 1], EPS, None, ALU.add).then_inc(s["var_ready"], 1)

            def apply(b):
                dve.wait_ge(s["rstd_ready"], b + 1)
                for t in range(NT):
                    dve.tensor_scalar(xn[:, t], x[:, t], mv[:, t, 0:1], rstd[:, t:t + 1], ALU.subtract, ALU.mult
                                      ).then_inc(s["xn_ready"], 1)

            def turned(b, k):
                dve.wait_ge(s["t_hi"], KC * b + k + 1)
                dve.tensor_tensor(xT[1][:, k, :], TB[k % 2][:], xT[0][:, k, :].bitcast(F32), ALU.subtract
                                  ).then_inc(s["t_lo"], 1)

            def split(b, m):
                r = m % 2
                dve.wait_ge(s["gelu"], MH * b + m + 1)
                dve.tensor_copy(hT[0][:, r, :], h32[:, r, :]).then_inc(s["h_hi"], 1)
                dve.wait_ge(s["h_hi"], MH * b + m + 1)
                dve.tensor_tensor(hT[1][:, r, :], h32[:, r, :], hT[0][:, r, :].bitcast(F32), ALU.subtract
                                  ).then_inc(s["h_lo"], 1)

            def finish(b):
                dve.wait_ge(s["x_biased"], NT * (b + 1))
                for t in range(NT):
                    dve.wait_ge(s["acc_ready"], NT * b + t + 1)
                    ins = dve.tensor_tensor(y[:, t], ACC[t][:], y[:, t], ALU.add)
                    ins.then_inc(s["acc_read"], 1)
                dve.wait_ge(s["acc_read"], NT * (b + 1) + 1)
                dve.sem_inc(s["out_ready"], 1)

            norm(0)
            for i in range(8):
                dve.wait_ge(s["w_hi"], i + 1)
                for k in range(4):
                    src = stages[i % 2][:, k, :]
                    hi = part_of(0, i)[:, k, :].bitcast(F32)
                    if i < 4:
                        ins = dve.scalar_tensor_tensor(out=part_of(1, i)[:, k, :], in0=src, scalar=ncol[:, 0, k:k + 1],
                                                       in1=hi, op0=ALU.mult, op1=ALU.subtract)
                    else:
                        ins = dve.tensor_tensor(part_of(1, i)[:, k, :], src, hi, ALU.subtract)
                ins.then_inc(s["w_lo"], 1)
            dve.wait_ge(s["bias_ps"], 4)
            dve.tensor_tensor(hb[:], F1[0][:, 0:MH], b1col[:], ALU.add).then_inc(s["bias_done"], 1)
            dve.wait_ge(s["w_lo"], 8)
            apply(0)
            for k in range(KC):
                turned(0, k)
            with dve.Fori(0, TURNS - 1) as b:
                for m in range(MH):
                    split(b, m)
                    if m == 8:
                        norm(b + 1)
                    if m == 10:
                        apply(b + 1)
                for k in range(KC):
                    turned(b + 1, k)
                finish(b)
            for m in range(MH):
                split(TURNS - 1, m)
            finish(TURNS - 1)

        @block.tensor
        def _(pe):
            pe.wait_ge(s["vec_loaded"], 4 * IT)
            for i in range(4):
                pe.wait_ge(s[f"stage_loaded{i % 2}"], IT * (i // 2 + 1))
                for j in range(4):
                    m = 4 * i + j
                    for k in range(KC):
                        ins = pe.matmul(F1[0][:, m:m + 1], stages[i % 2][:, k, j * P:(j + 1) * P], ncol[:, 1, k:k + 1],
                                        start=(k == 0), stop=(k == KC - 1))
                ins.then_inc(s["bias_ps"], 1)
            pe.wait_ge(s["pool_setup"], 1)

            def turn_over(b, k, first=False):
                if k == 0:
                    pe.wait_ge(s["xn_ready"], NT * (b + 1))
                if k >= 2:
                    pe.wait_ge(s["t_lo"], KC * b + k - 1)
                for t in range(NT):
                    ins = pe.transpose(TB[k % 2][:, t * P:(t + 1) * P], xn[:, t, k * P:(k + 1) * P], ident[:])
                ins.then_inc(s["t_ps"], 1)

            def hidden(b, m):
                product(pe, F1[m % 2][:], lambda k, a: W1[a][:, k, m * P:(m + 1) * P],
                        lambda k, p: xT[p][:, k, :]).then_inc(s["f1_ps"], 1)

            def down(b, m):
                pe.wait_ge(s["h_lo"], MH * b + m + 1)
                for t in range(NT):
                    if m == 0:
                        pe.wait_ge(s["acc_read"], NT * b + t + 1 if t == 0 else NT * b + 1)
                    for n, (a, p) in enumerate(PASSES):
                        ins = pe.matmul(ACC[t][:], hT[a][:, m % 2, t * P:(t + 1) * P], W2[p][:, m, :],
                                        start=(m == 0 and n == 0), stop=(m == MH - 1 and n == 2))
                    if m == MH - 1:
                        ins.then_inc(s["acc_ready"], 1)
                    elif t == NT - 1:
                        ins.then_inc(s["f2_step"], 1)

            def turn(b, last=False):
                for m in range(1, MH):
                    hidden(b, m)
                    down(b, m - 1)
                if not last:
                    for k in range(KC):
                        turn_over(b + 1, k)
                down(b, MH - 1)
                if not last:
                    pe.wait_ge(s["t_lo"], KC * (b + 2))
                    hidden(b + 1, 0)

            for k in range(KC):
                turn_over(0, k)
            pe.wait_ge(s["w_lo"], 8)
            pe.wait_ge(s["bias_done"], 1)
            pe.wait_ge(s["t_lo"], KC)
            hidden(0, 0)
            with pe.Fori(0, TURNS - 1) as b:
                turn(b)
            turn(TURNS - 1, last=True)


def two_layers(nc, a, out):
    x1 = nc.dram_tensor("after_attention0", [B, S, C], F32).ap()
    x2 = nc.dram_tensor("after_layer0", [B, S, C], F32).ap()
    x3 = nc.dram_tensor("after_attention1", [B, S, C], F32).ap()
    kv = a["L0_xattn_kv_w"]
    with nc.sbuf_tensor("rows_that_count", [P, B * TT], F32) as keep:
        attention_phase(nc, "mask", a["x"], a["ctx_1024"], a["mask_BxSxS2_bk0"], x1,
                        [a["L0_xattn_q_w"], kv[:, 0:C], kv[:, C:2 * C], a["L0_xattn_proj_w"]],
                        [a["L0_xattn_qn_w"], a["L0_xattn_qn_b"], a["L0_xattn_cn_w"], a["L0_xattn_cn_b"],
                         a["L0_xattn_proj_b"]], keep)
        mlp_phase(nc, x1, x2, a["L0_xattn_fc1_w"], a["L0_xattn_fc2_w"], a["L0_xattn_n2_w"], a["L0_xattn_n2_b"],
                  a["L0_xattn_fc1_b"], a["L0_xattn_fc2_b"])
        attention_phase(nc, "causal", x2, None, None, x3,
                        [a["L1_xattn_Wq1"], a["L1_xattn_Wk1"], a["L1_xattn_Wv1"]],
                        [a["L1_xattn_ln1_g"], a["L1_xattn_ln1_b"]], keep)
        attention_phase(nc, "cross", x3, a["ctx_1024"], None, out,
                        [a["L1_xattn_Wq2"], a["L1_xattn_Wk2"], a["L1_xattn_Wv2"], a["L1_xattn_fc1_w"],
                         a["L1_xattn_fc2_w"]],
                        [a["L1_xattn_ln2_g"], a["L1_xattn_ln2_b"], a["L1_xattn_fc1_b"], a["L1_xattn_fc2_b"],
                         a["L1_xattn_ln3_g"], a["L1_xattn_ln3_b"]], keep)


COLUMNS = ("L0_xattn_qn_w", "L0_xattn_qn_b", "L0_xattn_cn_w", "L0_xattn_cn_b", "L0_xattn_n2_w", "L0_xattn_n2_b",
           "L0_xattn_fc1_b", "L1_xattn_fc1_b")


def laid_out(name, a):
    a = np.asarray(a)
    if name.startswith("mask"):
        return np.ascontiguousarray(a)
    if "_Wq" in name or "_Wk" in name or "_Wv" in name:
        return np.ascontiguousarray(a.transpose(1, 0, 2)).reshape(C, C)
    if name in ("L1_xattn_fc1_w", "L1_xattn_fc2_w"):
        return np.ascontiguousarray(a.T)
    if name in COLUMNS:
        return np.ascontiguousarray(a.reshape(-1, P).T)
    return np.ascontiguousarray(a)


def kernel(**inputs):
    import concourse.bacc as _bacc
    from concourse.bass_utils import run_bass_kernel_spmd as _run

    nc = _bacc.Bacc("TRN2", target_bir_lowering=False, num_devices=1)
    arrays, args = {}, {}
    for name, value in inputs.items():
        v = laid_out(name, value)
        arrays[f"in_{name}"] = v
        args[name] = nc.dram_tensor(f"in_{name}", v.shape, mybir.dt.from_np(v.dtype), kind="ExternalInput").ap()
    out = nc.dram_tensor("out", [B, S, C], F32, kind="ExternalOutput").ap()
    two_layers(nc, args, out)
    r = _run(nc, [arrays], core_ids=[0])
    return r.results[0]["out"]
```
